# Optimizing a Trainium2 kernel written in Bass

```python
import numpy as np
import jax
import jax.numpy as jnp

def _softmax(x, axis=-1):
    return jax.nn.softmax(x, axis=axis)

def _gelu(x):
    return jax.nn.gelu(x, approximate=True)

def _silu(x):
    return jax.nn.silu(x)

def _sigmoid(x):
    return jax.nn.sigmoid(x)

def _layernorm(x, axis=-1, eps=1e-05):
    m = jnp.mean(x, axis=axis, keepdims=True)
    v = jnp.var(x, axis=axis, keepdims=True)
    return (x - m) / jnp.sqrt(v + eps)

def _scatter_add(tgt, idx, src, axis=0):
    return tgt.at[idx].add(src)

def _segment_sum(src, seg, n):
    return jax.ops.segment_sum(src, seg, n)
kernel_name = 'mk_flamingo_gated_d1_seqx_r8_ec5a22'

def setup_inputs(seed: int=0):
    np.random.seed(seed)
    _w = jnp.asarray

    def _rec_inputs():
        import jax
        import jax.numpy as jnp
        _rk = jax.random.key(seed)
        x = -0.0003929 + 0.9999 * jax.random.normal(jax.random.fold_in(_rk, 1), (8, 128, 512), jnp.float32)
        _lenS = 128 - jax.random.randint(jax.random.fold_in(_rk, 7), (8,), 0, max(1, 128 // 4) + 1, jnp.int32)
        _lenS2 = 128 - jax.random.randint(jax.random.fold_in(_rk, 8), (8,), 0, max(1, 128 // 4) + 1, jnp.int32)
        _ctx_4096P = jax.random.normal(jax.random.fold_in(_rk, 11), (8, 16, 512), jnp.float32)
        _ctx_4096c = jax.random.dirichlet(jax.random.fold_in(_rk, 511), 0.3 * jnp.ones((16,), jnp.float32), (8, 128))
        _ctx_4096t = jnp.einsum('bsk,bkd->bsd', _ctx_4096c, _ctx_4096P)
        _ctx_4096t = _ctx_4096t * jax.lax.rsqrt(jnp.mean(jnp.square(_ctx_4096t)) + 1e-12) * 0.953939
        ctx_4096 = 2.81802e-05 + 1.00001 * (_ctx_4096t + 0.3 * jax.random.normal(jax.random.fold_in(_rk, 611), (8, 128, 512), jnp.float32))
        pos_BxS2 = jnp.broadcast_to(jnp.arange(128, dtype=jnp.int32), (8, 128))
        _validS = jnp.arange(128)[None, :] < _lenS[:, None]
        _validS2 = jnp.arange(128)[None, :] < _lenS2[:, None]
        _causal = jnp.tril(jnp.ones((128, 128), dtype=bool))
        mask_BxSxS2_ik0 = jnp.where(jnp.broadcast_to(_validS2[:, None, :], (8, 128, 128)), 0, 1).astype(jnp.int32)
        _g = jax.random.normal(jax.random.fold_in(_rk, 9001), (2, 1), jnp.float32)
        _g = jnp.sign(_g) * jnp.maximum(jnp.abs(_g), 1.0) + (_g == 0) * 1.0
        g_xattn = _g[0]
        g_ffn = _g[1]
        return (x, ctx_4096, pos_BxS2, mask_BxSxS2_ik0, g_xattn, g_ffn)
    x, ctx_4096, pos_BxS2, mask_BxSxS2_ik0, g_xattn, g_ffn = _rec_inputs()

    def _L0_xattn_setup():
        import jax, jax.numpy as jnp
        import numpy as np
        B, S, E = (2, 256, 512)
        H, KVH, D = (32, 8, 128)
        GROUPS = H // KVH
        MAX_POS = 512
        ROPE_THETA = 10000.0

        def _rope_tables(max_pos, dim, theta):
            inv_freq = 1.0 / theta ** (jnp.arange(0, dim, 2, dtype=jnp.float32) / dim)
            t = jnp.arange(max_pos, dtype=jnp.float32)
            freqs = jnp.einsum('i,j->ij', t, inv_freq)
            emb = jnp.concatenate([freqs, freqs], axis=-1)
            return (jnp.cos(emb), jnp.sin(emb))

        def _rotate_half(x):
            x1, x2 = (x[..., :x.shape[-1] // 2], x[..., x.shape[-1] // 2:])
            return jnp.concatenate([-x2, x1], axis=-1)
        key = jax.random.key(seed)
        ks = jax.random.split(key, 8)
        scale_w = 1.0 / np.sqrt(E)
        query = jax.random.normal(ks[0], (B, S, E), dtype=jnp.float32)
        k_in = jax.random.normal(ks[1], (B, S, E), dtype=jnp.float32)
        v_in = jax.random.normal(ks[2], (B, S, E), dtype=jnp.float32)
        position_ids = jnp.broadcast_to(jnp.arange(S, dtype=jnp.int64), (B, S))
        src_mask = jnp.tril(jnp.ones((S, S), dtype=jnp.int32))
        src_mask = jnp.broadcast_to(src_mask, (B, S, S))
        Wq = jax.random.normal(ks[3], (E, H * D), dtype=jnp.float32) * scale_w
        Wk = jax.random.normal(ks[4], (E, KVH * D), dtype=jnp.float32) * scale_w
        Wv = jax.random.normal(ks[5], (E, KVH * D), dtype=jnp.float32) * scale_w
        Wo = jax.random.normal(ks[6], (H * D, E), dtype=jnp.float32) * scale_w
        return {'query': query, 'key': k_in, 'value': v_in, 'position_ids': position_ids, 'src_mask': src_mask, 'Wq': Wq, 'Wk': Wk, 'Wv': Wv, 'Wo': Wo}
    _L0_xattn_all = _L0_xattn_setup()
    _L0_xattn_in = {k: v for k, v in _L0_xattn_all.items() if k in ('Wq', 'Wk', 'Wv', 'Wo')}
    del _L0_xattn_all

    def _L0_ffn_setup():
        import jax, jax.numpy as jnp
        import numpy as np
        B, S, D = (4, 256, 512)
        NUM_EXPERTS, TOP_K = (3, 2)

        def _expert_outputs(h, w1, b1, w2, b2):
            pre = jnp.einsum('bsd,edf->ebsf', h, w1) + b1[:, None, None, :]
            act = jnp.stack([jnp.tanh(pre[0]), jax.nn.gelu(pre[1], approximate=False), jax.nn.silu(pre[2])])
            return jnp.einsum('ebsf,efd->ebsd', act, w2) + b2[:, None, None, :]
        key = jax.random.key(seed)
        ks = jax.random.split(key, 8)
        scale_in = 1.0 / np.sqrt(D)
        scale_gate = 1.0 / np.sqrt(D + 1)
        return {'h': jax.random.normal(ks[0], (B, S, D), dtype=jnp.float32), 'gate_w': jax.random.uniform(ks[1], (D + 1, NUM_EXPERTS), minval=-scale_gate, maxval=scale_gate, dtype=jnp.float32), 'gate_b': jnp.zeros((NUM_EXPERTS,), dtype=jnp.float32), 'w1': jax.random.uniform(ks[2], (NUM_EXPERTS, D, D), minval=-scale_in, maxval=scale_in, dtype=jnp.float32), 'b1': jnp.zeros((NUM_EXPERTS, D), dtype=jnp.float32), 'w2': jax.random.uniform(ks[3], (NUM_EXPERTS, D, D), minval=-scale_in, maxval=scale_in, dtype=jnp.float32), 'b2': jnp.zeros((NUM_EXPERTS, D), dtype=jnp.float32)}
    _L0_ffn_all = _L0_ffn_setup()
    _L0_ffn_in = {k: v for k, v in _L0_ffn_all.items() if k in ('gate_w', 'gate_b', 'w1', 'b1', 'w2', 'b2')}
    del _L0_ffn_all
    return {'x': x, 'ctx_4096': ctx_4096, 'pos_BxS2': pos_BxS2, 'mask_BxSxS2_ik0': mask_BxSxS2_ik0, 'g_xattn': g_xattn, 'g_ffn': g_ffn, 'L0_xattn_Wq': _L0_xattn_in['Wq'], 'L0_xattn_Wk': _L0_xattn_in['Wk'], 'L0_xattn_Wv': _L0_xattn_in['Wv'], 'L0_xattn_Wo': _L0_xattn_in['Wo'], 'L0_ffn_gate_w': _L0_ffn_in['gate_w'], 'L0_ffn_gate_b': _L0_ffn_in['gate_b'], 'L0_ffn_w1': _L0_ffn_in['w1'], 'L0_ffn_b1': _L0_ffn_in['b1'], 'L0_ffn_w2': _L0_ffn_in['w2'], 'L0_ffn_b2': _L0_ffn_in['b2']}

def reference(x, ctx_4096, pos_BxS2, mask_BxSxS2_ik0, g_xattn, g_ffn, L0_xattn_Wq, L0_xattn_Wk, L0_xattn_Wv, L0_xattn_Wo, L0_ffn_gate_w, L0_ffn_gate_b, L0_ffn_w1, L0_ffn_b1, L0_ffn_w2, L0_ffn_b2):
    import jax
    import jax.numpy as jnp

    def _L0_xattn_ref(query, key, value, position_ids, src_mask, Wq, Wk, Wv, Wo):
        import jax, jax.numpy as jnp
        import numpy as np
        B, S, E = (2, 256, 512)
        H, KVH, D = (32, 8, 128)
        GROUPS = H // KVH
        MAX_POS = 512
        ROPE_THETA = 10000.0

        def _rope_tables(max_pos, dim, theta):
            inv_freq = 1.0 / theta ** (jnp.arange(0, dim, 2, dtype=jnp.float32) / dim)
            t = jnp.arange(max_pos, dtype=jnp.float32)
            freqs = jnp.einsum('i,j->ij', t, inv_freq)
            emb = jnp.concatenate([freqs, freqs], axis=-1)
            return (jnp.cos(emb), jnp.sin(emb))

        def _rotate_half(x):
            x1, x2 = (x[..., :x.shape[-1] // 2], x[..., x.shape[-1] // 2:])
            return jnp.concatenate([-x2, x1], axis=-1)
        nb, q_len, _ = query.shape
        q = (query @ Wq).reshape(nb, q_len, H, D).transpose(0, 2, 1, 3)
        k = (key @ Wk).reshape(nb, q_len, KVH, D).transpose(0, 2, 1, 3)
        v = (value @ Wv).reshape(nb, q_len, KVH, D).transpose(0, 2, 1, 3)
        cos_t, sin_t = _rope_tables(MAX_POS, D, ROPE_THETA)
        cos = cos_t[position_ids][:, None]
        sin = sin_t[position_ids][:, None]
        q = q * cos + _rotate_half(q) * sin
        k = k * cos + _rotate_half(k) * sin
        k = jnp.repeat(k, GROUPS, axis=1)
        v = jnp.repeat(v, GROUPS, axis=1)
        scores = jnp.einsum('bhqd,bhkd->bhqk', q, k) / jnp.sqrt(jnp.float32(D))
        mask = src_mask[:, None]
        scores = jnp.where(mask == 0, jnp.float32(-1000000000.0), scores)
        attn = jax.nn.softmax(scores, axis=-1)
        x = jnp.einsum('bhqk,bhkd->bhqd', attn, v)
        x = x.transpose(0, 2, 1, 3).reshape(nb, q_len, H * D)
        return x @ Wo

    def _L0_ffn_ref(h, gate_w, gate_b, w1, b1, w2, b2):
        import jax, jax.numpy as jnp
        import numpy as np
        B, S, D = (4, 256, 512)
        NUM_EXPERTS, TOP_K = (3, 2)

        def _expert_outputs(h, w1, b1, w2, b2):
            pre = jnp.einsum('bsd,edf->ebsf', h, w1) + b1[:, None, None, :]
            act = jnp.stack([jnp.tanh(pre[0]), jax.nn.gelu(pre[1], approximate=False), jax.nn.silu(pre[2])])
            return jnp.einsum('ebsf,efd->ebsd', act, w2) + b2[:, None, None, :]
        b, s, d = h.shape
        vision_len = int(s * 0.3)
        text_strength = jnp.mean(jnp.abs(h[:, vision_len:, :]), axis=(1, 2), keepdims=True)
        vision_strength = jnp.mean(jnp.abs(h[:, :vision_len, :]), axis=(1, 2), keepdims=True)
        modality_ratio = text_strength / (vision_strength + 1e-08)
        modality_ratio = jnp.broadcast_to(modality_ratio, (b, s, 1))
        router_input = jnp.concatenate([h, modality_ratio], axis=-1)
        gate_logits = router_input @ gate_w + gate_b
        gate_scores = jax.nn.softmax(gate_logits, axis=-1)
        top_val, top_idx = jax.lax.top_k(gate_scores, TOP_K)
        top_val = top_val / (jnp.sum(top_val, axis=-1, keepdims=True) + 1e-08)
        expert_out = _expert_outputs(h, w1, b1, w2, b2)
        moe_out = jnp.zeros_like(h)
        batch_idx = jnp.arange(b)
        for i in range(TOP_K):
            j = top_idx[:, 0, i]
            out_i = expert_out[j, batch_idx]
            moe_out = moe_out + top_val[..., i:i + 1] * out_i
        return moe_out
    x = x + jnp.tanh(g_xattn[0]) * _L0_xattn_ref(_layernorm(x, axis=-1), ctx_4096, ctx_4096, pos_BxS2, mask_BxSxS2_ik0, L0_xattn_Wq, L0_xattn_Wk, L0_xattn_Wv, L0_xattn_Wo)
    x = x + jnp.tanh(g_ffn[0]) * _L0_ffn_ref(_layernorm(x, axis=-1), L0_ffn_gate_w, L0_ffn_gate_b, L0_ffn_w1, L0_ffn_b1, L0_ffn_w2, L0_ffn_b2)
    return x

_drawn_inputs = setup_inputs


def setup_inputs(seed=0):
    import zlib

    import numpy as np

    out = dict(_drawn_inputs(seed))
    spreads = {'L0_ffn_gate_b': (0.0, 0.316), 'L0_ffn_b1': (0.0, 0.542), 'L0_ffn_b2': (0.0, 0.1)}
    factors = {}
    for name, (base, spread) in spreads.items():
        noise = np.random.default_rng([zlib.crc32(name.encode()), seed]).standard_normal(out[name].shape)
        drawn = base * np.exp(spread * noise) if base else spread * noise
        out[name] = jnp.asarray(drawn.astype(out[name].dtype))
    for name, factor in factors.items():
        out[name] = (out[name] * factor).astype(out[name].dtype)
    return out
```

```python
from contextlib import ExitStack

import concourse.bass as bass
from concourse import mybir

ALU = mybir.AluOpType
ACT = mybir.ActivationFunctionType
AX = mybir.AxisListType
F32 = mybir.dt.float32
F32R = mybir.dt.float32r
I32 = mybir.dt.int32

P = 128
B = 8
E = 512
EC = E // P
H, KVH, D = 32, 8, 128
HG = H // KVH
GH = KVH // HG
HALF = D // 2
MAX_POS = 512
NX = 3
VISION = int(P * 0.3)
SCALE = float(D) ** -0.5
MASKED = -1.0e9
LN_EPS = 1e-5
KEEP = 3.0e38
UNITS = KVH * B
NROW = 4
NW = 4
NKV = 4
NST = 3
W_PER = 2 * EC
W_B = 4 * EC
W_C = W_B + KVH * W_PER


def build(nc, x, ctx_in, pos, mask, g_xattn, g_ffn, Wq, Wk, Wv, Wo, gate_w, gate_b, w1, b1, w2, b2,
          rope_rows, kv_scratch, out):
    with ExitStack() as stack:
        def sb(name, shape, dt=F32):
            return stack.enter_context(nc.sbuf_tensor(name, shape, dt))

        def bank(name):
            return stack.enter_context(nc.psum_tensor(name, [P, 512], F32))

        def sem(name):
            return stack.enter_context(nc.semaphore(name))

        xT = [sb(f"xT_{s}", [P, B, EC, P], F32R) for s in ("hi", "lo")]
        cT = [sb(f"cT_{s}", [P, B, EC, P], F32R) for s in ("hi", "lo")]
        wa = [[sb(f"wa{n}_{s}", [P, EC, 512], F32R) for s in ("hi", "lo")] for n in range(2)]
        wb = [[sb(f"wb{n}_{s}", [P, EC, 512], F32R) for s in ("hi", "lo")] for n in range(2)]
        wraw = sb("wraw", [P, NW, 512])
        split = sb("split", [P, NST, 2, 512], F32R)
        kv = sb("kv", [P, NKV, 4, P], F32R)
        xacc = sb("xacc", [P, B, E])
        rows = sb("rows", [P, NROW, E])
        rope = sb("rope", [P, B, 3 * HALF])
        limit = sb("limit", [P, B, P])
        rot = sb("rot", [P, 2, 512])
        roped = sb("roped", [P, 512])
        prob = sb("prob", [P, 2, 512])
        ident = sb("ident", [P, P])
        sel = sb("sel", [P, 3, P])
        posi = sb("posi", [P, B], I32)
        posf = sb("posf", [P, 3, B])
        gates = sb("gates", [P, 2])
        bn = sb("bn", [P, 2, B, 6])
        mv = sb("mv", [P, 2, B, 2])
        rstd = sb("rstd", [P, 2, B])
        mhalf = sb("mhalf", [P, B])
        nmax = sb("nmax", [P, 2, HG])
        psums = sb("psums", [P, 2, HG])
        prec = sb("prec", [P, 2, HG])
        gw = sb("gw", [P, EC, 4])
        gws = [sb(f"gws_{s}", [P, EC, 4], F32R) for s in ("hi", "lo")]
        gwm = sb("gwm", [P, 2, NX])
        b1c = sb("b1c", [P, NX, EC])
        absum = sb("absum", [P, B])
        r8 = sb("r8", [P, 12, B])
        lg = sb("lg", [P, 10, B, NX])
        coef = sb("coef", [P, B, NX])

        qbank = [bank("q0"), bank("q1")]
        tbank = bank("qt")
        sbank = bank("s")
        pbank = bank("pt")
        obank = bank("o")
        ybank = [bank("y0"), bank("y1")]
        trans = [pbank, obank]

        row_in = [sem(f"row_in{k}") for k in range(NROW)]
        x_in = [sem(f"x_in{b}") for b in range(B)]
        small_in = sem("small_in")
        pos_in = sem("pos_in")
        mask_in = sem("mask_in")
        w_in = [sem(f"w_in{k}") for k in range(NW)]
        w_hi, w_lo = sem("w_hi"), sem("w_lo")
        pool_const, ident_ok = sem("pool_const"), sem("ident_ok")
        pos_step, pos_ok = sem("pos_step"), sem("pos_ok")
        rope_in = sem("rope_in")
        lim_step, limit_ok = sem("lim_step"), sem("limit_ok")
        gates_ok = sem("gates_ok")
        ln_step, ln_var, ln_rstd, ln_row = sem("ln_step"), sem("ln_var"), sem("ln_rstd"), sem("ln_row")
        row_t, row_hi, row_lo = sem("row_t"), sem("row_hi"), sem("row_lo")
        k_proj, k_rot, k_roped, k_t = sem("k_proj"), sem("k_rot"), sem("k_roped"), sem("k_t")
        v_proj = sem("v_proj")
        u_hi, u_lo = sem("u_hi"), sem("u_lo")
        stored = [sem(f"stored{k}") for k in range(NST)]
        kv_in = [sem(f"kv_in{k}") for k in range(NKV)]
        q_proj, q_rot, q_roped, q_t = sem("q_proj"), sem("q_rot"), sem("q_roped"), sem("q_t")
        q_hi, q_lo = sem("q_hi"), sem("q_lo")
        s_done, s_limited, s_max, s_exp = sem("s_done"), sem("s_limited"), sem("s_max"), sem("s_exp")
        s_rec, p_norm, p_t, p_hi, p_lo = sem("s_rec"), sem("p_norm"), sem("p_t"), sem("p_hi"), sem("p_lo")
        o_done, o_hi, o_lo = sem("o_done"), sem("o_hi"), sem("o_lo")
        y_done, y_acc = sem("y_done"), sem("y_acc")
        h_step, h_var, h_rstd, h_row = sem("h_step"), sem("h_var"), sem("h_rstd"), sem("h_row")
        h_abs = sem("h_abs")
        h_t, h_hi, h_lo = sem("h_t"), sem("h_hi"), sem("h_lo")
        gw_hi, gw_lo = sem("gw_hi"), sem("gw_lo")
        route_mm, score_exp_in, score_exp, tok0_in, tok0_mm = (
            sem("route_mm"), sem("score_exp_in"), sem("score_exp"), sem("tok0_in"), sem("tok0_mm"))
        rt = sem("rt")
        coef_ok = sem("coef_ok")
        f1, f_act, f_hi, f_lo = sem("f1"), sem("f_act"), sem("f_hi"), sem("f_lo")
        f2, f_acc, f_bias = sem("f2"), sem("f_acc"), sem("f_bias")
        b2_in = sem("b2_in")
        out_done = sem("out_done")

        b2row = [rot[:, 0, :], rot[:, 1, :], roped[:, :]]

        ctx_rows = ctx_in
        w_chunks = []
        for half in range(GH):
            for m in (Wk, Wv):
                w_chunks += [m[c * P:(c + 1) * P, half * 512:(half + 1) * 512] for c in range(EC)]
        assert len(w_chunks) == W_B

        def w_target(n):
            if n < W_B:
                half, kind, c = n // (2 * EC), n // EC % 2, n % EC
                return (wa, wb)[kind][half], c
            kind, c = (n - W_B) // EC % 2, n % EC
            return (wa, wb)[kind][(n - W_B) // W_PER % 2], c

        def swap(ap):
            return ap.rearrange("p (h t d) -> p h t d", h=HG, t=2)[:, :, ::-1, :]

        def halves(ap):
            return ap.rearrange("p (h t d) -> p h t d", h=HG, t=2)

        def cos_of(b):
            return rope[:, b, 0:HALF].unsqueeze(1).unsqueeze(1).to_broadcast([P, HG, 2, HALF])

        def sin_of(b):
            return (rope[:, b, HALF:3 * HALF].rearrange("p (t d) -> p t d", t=2)
                    .unsqueeze(1).to_broadcast([P, HG, 2, HALF]))

        def heads(ap):
            return ap.rearrange("p (h k) -> p h k", h=HG)

        PASSES = ((0, 0), (0, 1), (1, 0))

        def project(pe, bank_, stationary, moving, chunks=EC):
            for c in range(chunks):
                for n, (s, m) in enumerate(PASSES):
                    mm = pe.matmul(bank_[:, :], stationary(s, c), moving(m, c),
                                   start=(c == 0 and n == 0), stop=(c == chunks - 1 and n == 2))
            return mm

        def groups(eng, unit):
            for b in range(B):
                unit(0, 0, b, b, False)
            with eng.Fori(1, KVH - 2, 2) as g:
                for par in (1, 0):
                    for b in range(B):
                        unit(g + (1 - par), par, b, B, False)
            for b in range(B):
                unit(KVH - 1, 1, b, B, False)
            for b in range(3):
                unit(KVH, 0, b, B, True)

        def lagged(par, b, lag):
            return (par if b >= lag else 1 - par), (b - lag) % B

        def is_last(g, b):
            return isinstance(g, int) and g == KVH - 1

        def acts(a, s):
            return cT[a][:, (s % 2) * 4:(s % 2) * 4 + 4, :, :].rearrange("p b c t -> p b (c t)")

        def bcast(row, n):
            return row.rearrange("(a n) -> a n", a=1).to_broadcast([P, n])

        def store(sp, m):
            half, kind, b = m // (2 * B), m // B % 2, m % B
            sp.wait_ge(u_lo, m + 1)
            for s in range(2):
                sp.dma_start(kv_scratch[half * HG:(half + 1) * HG, b, :, 2 * kind + s, :]
                             .rearrange("g p k -> p g k"),
                             heads(split[:, m % NST, s, :].bitcast(F32))).then_inc(stored[m % NST], 16)

        block = stack.enter_context(nc.Block())

        @block.sync
        def _(sp):
            def w_load(n, src):
                if n >= NW:
                    sp.wait_ge(w_lo, n - NW + 1)
                return sp.dma_start(wraw[:, n % NW, :], src)

            sp.dma_start(rows[:, 0, :], ctx_rows[0]).then_inc(row_in[0], 16)
            for n in range(NW):
                w_load(n, w_chunks[n]).then_inc(w_in[n], 16)
            sp.dma_start(posi[:, :], pos.rearrange("b s -> s b"), allow_slow_non_contiguous=True).then_inc(pos_in, 16)
            for t in range(1, NROW):
                sp.dma_start(rows[:, t, :], ctx_rows[t]).then_inc(row_in[t], 16)
            for b in range(B):
                sp.dma_start(xacc[:, b, :], x[b]).then_inc(x_in[b], 16)
            sp.dma_start(prob[:, :, :].bitcast(I32).rearrange("p t (b k) -> p (t b) k", b=HG),
                         mask.rearrange("b q k -> q b k")).then_inc(mask_in, 16)
            sp.dma_start(gates[:, 0:1], bcast(g_xattn, 1)).then_inc(small_in, 16)
            sp.dma_start(gates[:, 1:2], bcast(g_ffn, 1)).then_inc(small_in, 16)
            sp.dma_start(gwm[:, 0, :], bcast(gate_w[E, :], NX)).then_inc(small_in, 16)
            sp.dma_start(gwm[:, 1, :], bcast(gate_b, NX)).then_inc(small_in, 16)
            sp.wait_ge(pool_const, 1)
            sp.dma_start(gw[:, :, 0:NX], gate_w[0:E, :].rearrange("(c p) e -> p c e", p=P),
                         allow_slow_non_contiguous=True).then_inc(small_in, 16)
            for e in range(NX):
                sp.dma_start(b1c[:, e, :], b1[e].rearrange("(c p) -> p c", p=P),
                             allow_slow_non_contiguous=True).then_inc(small_in, 16)

            for m in range(4 * B):
                if m + NROW < B:
                    t = m + NROW
                    sp.wait_ge(row_t, t - NROW + 1)
                    sp.dma_start(rows[:, t % NROW, :], ctx_rows[t]).then_inc(row_in[t % NROW], 16)
                n = NW + m
                if n < W_B:
                    w_load(n, w_chunks[n]).then_inc(w_in[n % NW], 16)
                elif n < W_B + W_PER:
                    k = n - W_B
                    src = (Wq[k * P:(k + 1) * P, 0:512] if k < EC else Wo[(k - EC) * P:(k - EC + 1) * P, :])
                    w_load(n, src).then_inc(w_in[n % NW], 16)
                if m >= 1:
                    store(sp, m - 1)
            store(sp, 4 * B - 1)

            for k in range(NST):
                sp.wait_ge(stored[k], 32 * len(range(k, 4 * B, NST)))

            def unit(g, par, b, past, drain):
                if drain:
                    return
                i = g * B + b
                if past >= NKV:
                    sp.wait_ge(o_done, i - NKV + 1)
                sp.dma_start(kv[:, b % NKV, :, :].bitcast(F32), kv_scratch[g, b]).then_inc(kv_in[b % NKV], 16)
                n = g * W_PER + (W_B + W_PER + b)
                sp.wait_ge(w_lo, n - NW + 1)
                last = isinstance(g, int) and g == KVH - 1
                if last:
                    src = w1[0, b * P:(b + 1) * P, :] if b < EC else w2[0, (b - EC) * P:(b - EC + 1) * P, :]
                elif b < EC:
                    src = Wq[b * P:(b + 1) * P, bass.ds(g * 512 + 512, 512)]
                else:
                    src = Wo[bass.ds(g * 512 + (512 + (b - EC) * P), P), :]
                sp.dma_start(wraw[:, b % NW, :], src).then_inc(w_in[b % NW], 16)

            groups(sp, unit)

            sp.wait_ge(q_roped, UNITS)
            sp.wait_ge(q_t, UNITS)
            for e in range(NX):
                sp.dma_start(b2row[e], bcast(b2[e], E)).then_inc(b2_in, 16)
            for e in range(1, NX):
                for k in range(W_PER):
                    n = W_C + e * W_PER + k
                    w_load(n, w1[e, k * P:(k + 1) * P, :] if k < EC else w2[e, (k - EC) * P:(k - EC + 1) * P, :]
                           ).then_inc(w_in[n % NW], 16)
            for b in range(B):
                sp.wait_ge(f_acc, (NX - 1) * B + b + 1)
                sp.dma_start(out[b], xacc[:, b, :]).then_inc(out_done, 16)
            sp.wait_ge(out_done, 16 * B)

        @block.tensor
        def _(pe):
            def transpose4(bank_, src, done):
                for c in range(4):
                    mm = pe.transpose(bank_[:, c * P:(c + 1) * P], src(c), ident[:, :])
                mm.then_inc(done, 1)

            def row_transpose(t):
                if t < B:
                    pe.wait_ge(row_in[t % NROW], 16 * (t // NROW + 1))
                else:
                    pe.wait_ge(ln_row, t - B + 1)
                if t >= 2:
                    pe.wait_ge(row_lo, t - 1)
                transpose4(trans[t % 2], lambda c: rows[:, t % NROW, c * P:(c + 1) * P], row_t)

            pe.wait_ge(ident_ok, 2)
            row_transpose(0)
            row_transpose(1)
            for m in range(4 * B):
                half, kind, b = m // (2 * B), m // B % 2, m % B
                if m < B:
                    pe.wait_ge(row_lo, m + 1)
                if b == 0:
                    pe.wait_ge(w_lo, (2 * half + kind + 1) * EC)
                if kind == 0:
                    k = half * B + b
                    if k >= 2:
                        pe.wait_ge(k_rot, k - 1)
                    project(pe, qbank[k % 2], lambda s, c: cT[s][:, b, c, :],
                            lambda s, c: wa[half][s][:, c, :]).then_inc(k_proj, 1)
                else:
                    v = half * B + b
                    if v >= 2:
                        pe.wait_ge(u_lo, m - 1)
                    project(pe, ybank[v % 2], lambda s, c: cT[s][:, b, c, :],
                            lambda s, c: wb[half][s][:, c, :]).then_inc(v_proj, 1)
                if m + 2 < B:
                    row_transpose(m + 2)
                elif B <= m < 2 * B:
                    row_transpose(m)
                if m >= 1 and (m - 1) // B % 2 == 0:
                    k = (m - 1) // (2 * B) * B + (m - 1) % B
                    pe.wait_ge(k_roped, k + 1)
                    if m >= 2:
                        pe.wait_ge(u_lo, m - 1)
                    transpose4(tbank, lambda c: roped[:, c * P:(c + 1) * P], k_t)

            pe.wait_ge(row_lo, 2 * B)

            def unit(g, par, b, past, drain):
                i = g * B + b

                def has(lag):
                    return past >= lag and (not drain or b < lag)

                if has(1):
                    pe.wait_ge(q_roped, i)
                    if past >= 2:
                        pe.wait_ge(q_lo, i - 1)
                    if (is_last(g, b) and b >= 5) or drain:
                        pe.wait_ge(h_lo, b - 4 if not drain else b + 4)
                    transpose4(tbank, lambda c: roped[:, c * P:(c + 1) * P], q_t)
                if has(0):
                    if b == 0:
                        pe.wait_ge(w_lo, g * W_PER + (W_B + EC))
                    if past >= 2:
                        pe.wait_ge(q_rot, i - 1)
                    project(pe, qbank[b % 2], lambda s, c: xT[s][:, b, c, :],
                            lambda s, c: wa[par][s][:, c, :]).then_inc(q_proj, 1)
                if has(2):
                    pe.wait_ge(p_norm, i - 1)
                    if past >= 3:
                        pe.wait_ge(p_lo, i - 2)
                    transpose4(pbank, lambda c: prob[:, 1, c * P:(c + 1) * P], p_t)
                if has(1):
                    p1, b1_ = lagged(par, b, 1)
                    pe.wait_ge(q_lo, i)
                    pe.wait_ge(kv_in[b1_ % NKV], (g * 2 + ((b - 1) // NKV + 1)) * 16)
                    if past >= 2:
                        pe.wait_ge(s_exp, i - 1)
                    for h in range(HG):
                        for n, (s, m) in enumerate(PASSES):
                            mm = pe.matmul(sbank[:, h * P:(h + 1) * P], split[:, 0, s, h * P:(h + 1) * P],
                                           kv[:, b1_ % NKV, m, :], start=(n == 0), stop=(n == 2))
                    mm.then_inc(s_done, 1)
                if has(3):
                    p3, b3 = lagged(par, b, 3)
                    pe.wait_ge(o_lo, i - 2)
                    if b3 == 0:
                        pe.wait_ge(w_lo, g * W_PER + (W_B + W_PER))
                    if past >= 5:
                        pe.wait_ge(y_acc, i - 4)
                    project(pe, ybank[b3 % 2], lambda s, c: split[:, 2, s, c * P:(c + 1) * P],
                            lambda s, c: wb[p3][s][:, c, :]).then_inc(y_done, 1)
                if is_last(g, b) or drain:
                    hb = b - 4 if not drain else b + 4
                    if hb >= 0:
                        h_transpose(hb)
                if has(2):
                    p2, b2_ = lagged(par, b, 2)
                    pe.wait_ge(p_lo, i - 1)
                    if past >= 3:
                        pe.wait_ge(o_lo, i - 2)
                    for n, (s, m) in enumerate(PASSES):
                        mm = pe.matmul(obank[:, :], kv[:, b2_ % NKV, 2 + s, :], split[:, 1, m, :],
                                       start=(n == 0), stop=(n == 2))
                    mm.then_inc(o_done, 1)

            def h_transpose(hb):
                pe.wait_ge(h_row, hb + 1)
                pe.wait_ge(q_lo, min(UNITS, UNITS - B + hb + 4))
                if hb >= 1:
                    pe.wait_ge(h_lo, hb)
                transpose4(tbank, lambda c: rows[:, hb % NROW, c * P:(c + 1) * P], h_t)

            groups(pe, unit)
            h_transpose(B - 1)

            def first_layer(s):
                e, hf = s // 2, s % 2
                if hf == 0:
                    pe.wait_ge(w_lo, W_C + e * W_PER + EC)
                for f in range(EC):
                    l = s * EC + f
                    if l < 2:
                        pe.wait_ge(q_rot, UNITS)
                    else:
                        pe.wait_ge(f_act, l - 1)
                    for c in range(EC):
                        for n, (a, m) in enumerate(PASSES):
                            mm = pe.matmul(qbank[l % 2][:, :], wa[e % 2][a][:, c, f * P:(f + 1) * P],
                                           xT[m][:, hf * 4:hf * 4 + 4, c, :],
                                           start=(c == 0 and n == 0), stop=(c == EC - 1 and n == 2))
                    mm.then_inc(f1, 1)

            def second_layer(s):
                e, hf = s // 2, s % 2
                if hf == 0:
                    pe.wait_ge(w_lo, W_C + (e + 1) * W_PER)
                pe.wait_ge(f_lo, (s + 1) * EC)
                for k in range(4):
                    u = s * 4 + k
                    if u < 2:
                        pe.wait_ge(y_acc, UNITS - 1 + u)
                    else:
                        pe.wait_ge(f_acc, u - 1)
                    project(pe, ybank[u % 2],
                            lambda a, c: acts(a, s)[:, c, k * P:(k + 1) * P],
                            lambda a, c: wb[e % 2][a][:, c, :]).then_inc(f2, 1)

            def router():
                pe.wait_ge(gw_lo, 1)
                pe.wait_ge(h_abs, B)
                pe.wait_ge(s_exp, UNITS)
                for b in range(B):
                    for c in range(EC):
                        for n, (a, m) in enumerate(PASSES):
                            pe.matmul(sbank[:, 4 * b:4 * b + 4], xT[a][:, b, c, :], gws[m][:, c, :],
                                      start=(c == 0 and n == 0), stop=(c == EC - 1 and n == 2))
                for k in range(2):
                    mm = pe.matmul(sbank[:, 64 + B * k:64 + B * (k + 1)], sel[:, k, :], absum[:, :],
                                   start=True, stop=True)
                mm.then_inc(route_mm, 1)

            def token0():
                pe.wait_ge(tok0_in, 1)
                pe.matmul(sbank[:, 128:128 + B * NX], sel[:, 2, :], lg[:, 4, :, :].rearrange("p b e -> p (b e)"),
                          start=True, stop=True).then_inc(tok0_mm, 1)

            pe.wait_ge(h_lo, 4)
            pe.wait_ge(h_lo, B)
            router()
            first_layer(0)
            token0()
            for s in range(1, 2 * NX):
                first_layer(s)
                second_layer(s - 1)
            second_layer(2 * NX - 1)

        @block.scalar
        def _(act):
            def w_split_hi(n, k, dst):
                act.wait_ge(w_in[k], (n // NW + 1) * 16)
                act.activation(dst, wraw[:, k, :], ACT.Copy).then_inc(w_hi, 1)

            def row_hi_(t):
                act.wait_ge(row_t, t + 1)
                dst = (cT if t < B else xT)[0][:, t % B, :, :]
                act.activation(dst.rearrange("p c t -> p (c t)"), trans[t % 2][:, :], ACT.Copy).then_inc(row_hi, 1)

            def unit_hi(m):
                if m >= NST:
                    act.wait_ge(stored[m % NST], 32 * (m // NST))
                half, kind, b = m // (2 * B), m // B % 2, m % B
                k = half * B + b
                if kind == 0:
                    act.wait_ge(k_t, k + 1)
                    act.activation(split[:, m % NST, 0, :], tbank[:, :], ACT.Copy, scale=SCALE).then_inc(u_hi, 1)
                else:
                    act.wait_ge(v_proj, k + 1)
                    act.activation(split[:, m % NST, 0, :], ybank[k % 2][:, :], ACT.Copy).then_inc(u_hi, 1)

            for n in range(EC):
                buf, c = w_target(n)
                w_split_hi(n, n % NW, buf[0][:, c, :])
                if n < 2:
                    row_hi_(n)
            for m in range(4 * B):
                if m + 2 < B:
                    row_hi_(m + 2)
                elif B <= m < 2 * B:
                    row_hi_(m)
                n = EC + m
                if n < W_B + W_PER:
                    if n == W_B:
                        act.wait_ge(k_proj, B)
                    if n == W_B + EC:
                        act.wait_ge(v_proj, B)
                    buf, c = w_target(n)
                    w_split_hi(n, n % NW, buf[0][:, c, :])
                if m >= 1 and (m - 1) // B % 2 == 0:
                    unit_hi(m - 1)
                if m // B % 2 == 1:
                    unit_hi(m)
            act.wait_ge(small_in, 16 * 8)
            act.activation(gates[:, :], gates[:, :], ACT.Tanh).then_inc(gates_ok, 1)
            act.activation(gws[0][:, :, :], gw[:, :, :], ACT.Copy).then_inc(gw_hi, 1)

            for k in range(NST):
                act.wait_ge(stored[k], 32 * len(range(k, 4 * B, NST)))

            def unit(g, par, b, past, drain):
                i = g * B + b

                def has(lag):
                    return past >= lag and (not drain or b < lag)

                if has(3):
                    act.wait_ge(o_done, i - 2)
                    if past >= 4:
                        act.wait_ge(y_done, i - 3)
                    act.activation(split[:, 2, 0, :], obank[:, :], ACT.Copy).then_inc(o_hi, 1)
                if has(1):
                    act.wait_ge(q_t, i)
                    if past >= 2:
                        act.wait_ge(s_done, i - 1)
                    act.activation(split[:, 0, 0, :], tbank[:, :], ACT.Copy).then_inc(q_hi, 1)
                if has(0):
                    nxt = 1 - par
                    if b == 0:
                        if past >= B:
                            act.wait_ge(q_proj, g * B)
                        else:
                            act.wait_ge(k_proj, 2 * B)
                    if b == EC:
                        if past >= B:
                            act.wait_ge(y_done, g * B)
                        else:
                            act.wait_ge(v_proj, 2 * B)
                    buf = (wa if b < EC else wb)[nxt]
                    act.wait_ge(w_in[b % NW], (g * 2 + (W_B + W_PER + b) // NW + 1) * 16)
                    act.activation(buf[0][:, b % EC, :], wraw[:, b % NW, :], ACT.Copy).then_inc(w_hi, 1)
                if has(2):
                    act.wait_ge(p_t, i - 1)
                    if past >= 3:
                        act.wait_ge(o_done, i - 2)
                    act.activation(split[:, 1, 0, :], pbank[:, :], ACT.Copy).then_inc(p_hi, 1)
                if has(1):
                    act.wait_ge(s_max, i)
                    if past >= 2:
                        act.wait_ge(p_norm, i - 1)
                    q1 = (b - 1) % 2
                    for h in range(HG):
                        a = act.activation(prob[:, 0, h * P:(h + 1) * P], sbank[:, h * P:(h + 1) * P], ACT.Exp,
                                           bias=nmax[:, q1, h:h + 1], accum_out=psums[:, q1, h:h + 1])
                    a.then_inc(s_exp, 1)
                if is_last(g, b) or drain:
                    hb = b - 4 if not drain else b + 4
                    if hb >= 0:
                        h_hi_(hb)

            def h_hi_(hb):
                act.wait_ge(h_t, hb + 1)
                act.wait_ge(q_proj, UNITS - B + hb + 1)
                act.activation(xT[0][:, hb, :, :].rearrange("p c t -> p (c t)"), tbank[:, :], ACT.Copy
                               ).then_inc(h_hi, 1)

            groups(act, unit)
            h_hi_(B - 1)

            def expert_weights(e):
                for k in range(W_PER):
                    n = W_C + e * W_PER + k
                    if k == 0:
                        if e == 1:
                            act.wait_ge(q_proj, UNITS)
                        else:
                            act.wait_ge(f1, (e - 1) * 2 * EC)
                    if k == EC:
                        if e == 1:
                            act.wait_ge(y_done, UNITS)
                        else:
                            act.wait_ge(f2, (e - 1) * B)
                    buf, c = (wa if k < EC else wb)[e % 2], k % EC
                    w_split_hi(n, n % NW, buf[0][:, c, :])

            def activations(s):
                for f in range(EC):
                    l, e = s * EC + f, s // 2
                    act.wait_ge(f1, l + 1)
                    if l < 2:
                        act.wait_ge(p_t, UNITS)
                    if l >= 2:
                        act.wait_ge(f_lo, l - 1)
                    func = (ACT.Tanh, ACT.Gelu, ACT.Silu)[e]
                    act.activation(prob[:, l % 2, :], qbank[l % 2][:, :], func, bias=b1c[:, e, f:f + 1]
                                   ).then_inc(f_act, 1)
                    act.wait_ge(f_act, l + 1)
                    if s >= 2 and f == 0:
                        act.wait_ge(f2, (s - 1) * 4)
                    act.activation(acts(0, s)[:, f, :], prob[:, l % 2, :], ACT.Copy).then_inc(f_hi, 1)

            act.wait_ge(score_exp_in, 1)
            act.activation(lg[:, 1, :, :], lg[:, 0, :, :], ACT.Exp).then_inc(score_exp, 1)
            activations(0)
            expert_weights(1)
            activations(1)
            activations(2)
            expert_weights(2)
            for s in range(3, 2 * NX):
                activations(s)

        @block.gpsimd
        def _(pool):
            pool.memset(gw[:, :, :], 0.0).then_inc(pool_const, 1)
            pool.memset(ident[:, :], 0.0).then_inc(ident_ok, 1)
            pool.wait_ge(ident_ok, 1)
            pool.affine_select(out=ident[:, :], in_=ident[:, :], compare_op=ALU.not_equal, fill=1.0, base=0,
                               pattern=[[-1, P]], channel_multiplier=1).then_inc(ident_ok, 1)
            pool.memset(mhalf[:, :], -0.5).then_inc(pool_const, 1)
            pool.memset(sel[:, :, :], 1.0).then_inc(pool_const, 1)
            pool.wait_ge(pool_const, 3)
            pool.affine_select(out=sel[:, 0, :], in_=sel[:, 0, :], compare_op=ALU.is_ge, fill=0.0, base=-VISION,
                               pattern=[[0, P]], channel_multiplier=1).then_inc(pool_const, 1)
            pool.affine_select(out=sel[:, 1, :], in_=sel[:, 1, :], compare_op=ALU.is_gt, fill=0.0, base=VISION,
                               pattern=[[0, P]], channel_multiplier=-1).then_inc(pool_const, 1)
            pool.affine_select(out=sel[:, 2, :], in_=sel[:, 2, :], compare_op=ALU.is_gt, fill=0.0, base=1,
                               pattern=[[0, P]], channel_multiplier=-1).then_inc(pool_const, 1)

            pool.wait_ge(pos_ok, 1)
            for b in range(B):
                pool.indirect_dma_start(rope[:, b, :], None, rope_rows[:, :],
                                        bass.IndirectOffsetOnAxis(ap=posi[:, b:b + 1], axis=0)
                                        ).then_inc(rope_in, 16)

            def w_split_lo(n, dst):
                pool.wait_ge(w_hi, n + 1)
                pool.tensor_tensor(dst[1], wraw[:, n % NW, :], dst[0].bitcast(F32), ALU.subtract).then_inc(w_lo, 1)

            for n in range(EC):
                buf, c = w_target(n)
                w_split_lo(n, [buf[s][:, c, :] for s in range(2)])
            for m in range(4 * B):
                n = EC + m
                if n < W_B + W_PER:
                    buf, c = w_target(n)
                    w_split_lo(n, [buf[s][:, c, :] for s in range(2)])
                if m // B % 2 == 0:
                    k = m // (2 * B) * B + m % B
                    pool.wait_ge(k_rot, k + 1)
                    if k >= 1:
                        pool.wait_ge(k_t, k)
                    pool.tensor_tensor(roped[:, :], rot[:, 0, :], rot[:, 1, :], ALU.add).then_inc(k_roped, 1)
                if m == B - 1:
                    pool.wait_ge(ln_var, 1)
                    pool.tensor_tensor(rstd[:, 0, :], rstd[:, 0, :], mhalf[:, :], ALU.pow).then_inc(ln_rstd, 1)

            pool.wait_ge(k_t, 2 * B)

            def unit(g, par, b, past, drain):
                i = g * B + b

                def has(lag):
                    return past >= lag and (not drain or b < lag)

                if has(0):
                    nxt = 1 - par
                    buf = (wa if b < EC else wb)[nxt]
                    pool.wait_ge(w_hi, g * W_PER + (W_B + W_PER + b + 1))
                    pool.tensor_tensor(buf[1][:, b % EC, :], wraw[:, b % NW, :],
                                       buf[0][:, b % EC, :].bitcast(F32), ALU.subtract).then_inc(w_lo, 1)
                    pool.wait_ge(q_rot, i + 1)
                    if past >= 1:
                        pool.wait_ge(q_t, i)
                    pool.tensor_tensor(roped[:, :], rot[:, 0, :], rot[:, 1, :], ALU.add).then_inc(q_roped, 1)
                if has(1):
                    q1 = (b - 1) % 2
                    pool.wait_ge(s_rec, i)
                    if past >= 2:
                        pool.wait_ge(p_t, i - 1)
                    pool.tensor_tensor(heads(prob[:, 1, :]), heads(prob[:, 0, :]),
                                       prec[:, q1, :].unsqueeze(2).to_broadcast([P, HG, P]), ALU.mult
                                       ).then_inc(p_norm, 1)
                if is_last(g, b) or drain:
                    hb = b - 3 if not drain else b + 5
                    if hb >= 0:
                        pool.wait_ge(h_var, hb + 1)
                        pool.tensor_tensor(rstd[:, 1, hb:hb + 1], rstd[:, 1, hb:hb + 1], mhalf[:, 0:1], ALU.pow
                                           ).then_inc(h_rstd, 1)

            groups(pool, unit)

            for e in range(1, NX):
                for k in range(W_PER):
                    n = W_C + e * W_PER + k
                    buf, c = (wa if k < EC else wb)[e % 2], k % EC
                    w_split_lo(n, [buf[s][:, c, :] for s in range(2)])

        @block.vector
        def _(dve):
            def subtract_hi(dst, src, hi, done):
                dve.tensor_tensor(dst, src, hi.bitcast(F32), ALU.subtract).then_inc(done, 1)

            def row_lo_(t):
                dve.wait_ge(row_hi, t + 1)
                T = cT if t < B else xT
                subtract_hi(T[1][:, t % B, :, :].rearrange("p c t -> p (c t)"), trans[t % 2][:, :],
                            T[0][:, t % B, :, :].rearrange("p c t -> p (c t)"), row_lo)

            def unit_lo(m):
                half, kind, b = m // (2 * B), m // B % 2, m % B
                k = half * B + b
                dve.wait_ge(u_hi, m + 1)
                hi, lo = split[:, m % NST, 0, :], split[:, m % NST, 1, :]
                if kind == 0:
                    dve.scalar_tensor_tensor(out=lo, in0=tbank[:, :], scalar=SCALE, in1=hi.bitcast(F32),
                                             op0=ALU.mult, op1=ALU.subtract).then_inc(u_lo, 1)
                else:
                    subtract_hi(lo, ybank[k % 2][:, :], hi, u_lo)

            def rotate(bank_, b, done):
                dve.tensor_tensor(halves(rot[:, 0, :]), halves(bank_[:, :]), cos_of(b), ALU.mult)
                dve.tensor_tensor(halves(rot[:, 1, :]), swap(bank_[:, :]), sin_of(b), ALU.mult).then_inc(done, 1)

            dve.wait_ge(pos_in, 16)
            dve.tensor_copy(posf[:, 0, :], posi[:, :]).then_inc(pos_step, 1)
            dve.wait_ge(pos_step, 1)
            dve.tensor_scalar(posf[:, 1, :], posf[:, 0, :], 0.0, float(MAX_POS), ALU.is_lt, ALU.mult
                              ).then_inc(pos_step, 1)
            dve.wait_ge(pos_step, 2)
            dve.tensor_tensor(posf[:, 2, :], posf[:, 0, :], posf[:, 1, :], ALU.add).then_inc(pos_step, 1)
            dve.wait_ge(pos_step, 3)
            dve.tensor_scalar(posi[:, :], posf[:, 2, :], 0.0, float(MAX_POS - 1), ALU.max, ALU.min
                              ).then_inc(pos_ok, 1)

            row_lo_(0)
            row_lo_(1)
            for m in range(4 * B):
                if m + 2 < B:
                    row_lo_(m + 2)
                elif B <= m < 2 * B:
                    row_lo_(m)
                if m >= 1 and (m - 1) // B % 2 == 0:
                    unit_lo(m - 1)
                if m // B % 2 == 0:
                    k = m // (2 * B) * B + m % B
                    if k == 0:
                        dve.wait_ge(rope_in, 16 * B)
                    dve.wait_ge(k_proj, k + 1)
                    if k >= 1:
                        dve.wait_ge(k_roped, k)
                    rotate(qbank[k % 2], m % B, k_rot)
                else:
                    unit_lo(m)
                if m < B:
                    dve.wait_ge(x_in[m], 16)
                    dve.bn_stats(bn[:, 0, m, :], xacc[:, m, :]).then_inc(ln_step, 1)
                    dve.wait_ge(ln_step, 2 * m + 1)
                    dve.bn_aggr(mv[:, 0, m, :], bn[:, 0, m, :]).then_inc(ln_step, 1)
                if m == B - 2 + 1:
                    dve.wait_ge(ln_step, 2 * B)
                    dve.tensor_scalar(rstd[:, 0, :], mv[:, 0, :, 1], LN_EPS, None, ALU.add).then_inc(ln_var, 1)
                    dve.wait_ge(ln_rstd, 1)
                if B - 1 <= m < 2 * B - 1:
                    b = m - (B - 1)
                    dve.wait_ge(row_t, B + b - NROW + 1)
                    dve.tensor_scalar(rows[:, b % NROW, :], xacc[:, b, :], mv[:, 0, b, 0:1], rstd[:, 0, b:b + 1],
                                      ALU.subtract, ALU.mult).then_inc(ln_row, 1)
                if m == 2 * B:
                    raw = prob[:, :, :].bitcast(I32).rearrange("p t (b k) -> p (t b) k", b=HG)
                    dve.wait_ge(mask_in, 16)
                    dve.tensor_scalar(limit[:, :, :], raw, 0.0, MASKED, ALU.is_equal, ALU.mult).then_inc(lim_step, 1)
                    dve.tensor_scalar(prob[:, :, :].rearrange("p t (b k) -> p (t b) k", b=HG), raw,
                                      0.0, KEEP, ALU.not_equal, ALU.mult).then_inc(lim_step, 1)
                    dve.wait_ge(lim_step, 2)
                    dve.tensor_tensor(limit[:, :, :], limit[:, :, :],
                                      prob[:, :, :].rearrange("p t (b k) -> p (t b) k", b=HG), ALU.add
                                      ).then_inc(limit_ok, 1)
            dve.wait_ge(gw_hi, 1)
            subtract_hi(gws[1][:, :, :], gw[:, :, :], gws[0][:, :, :], gw_lo)
            dve.wait_ge(gates_ok, 1)
            dve.wait_ge(limit_ok, 1)
            for k in range(NST):
                dve.wait_ge(stored[k], 32 * len(range(k, 4 * B, NST)))
            dve.wait_ge(k_roped, 2 * B)

            def unit(g, par, b, past, drain):
                i = g * B + b

                def has(lag):
                    return past >= lag and (not drain or b < lag)

                if has(3):
                    dve.wait_ge(o_hi, i - 2)
                    subtract_hi(split[:, 2, 1, :], obank[:, :], split[:, 2, 0, :], o_lo)
                if has(1):
                    dve.wait_ge(q_hi, i)
                    subtract_hi(split[:, 0, 1, :], tbank[:, :], split[:, 0, 0, :], q_lo)
                if has(0):
                    dve.wait_ge(q_proj, i + 1)
                    if past >= 1:
                        dve.wait_ge(q_roped, i)
                    rotate(qbank[b % 2], b, q_rot)
                if has(2):
                    dve.wait_ge(p_hi, i - 1)
                    subtract_hi(split[:, 1, 1, :], pbank[:, :], split[:, 1, 0, :], p_lo)
                if has(1):
                    q1, b1_ = (b - 1) % 2, (b - 1) % B
                    dve.wait_ge(s_done, i)
                    dve.tensor_tensor(heads(sbank[:, :]), heads(sbank[:, :]),
                                      limit[:, b1_, :].unsqueeze(1).to_broadcast([P, HG, P]), ALU.min
                                      ).then_inc(s_limited, 1)
                    dve.wait_ge(s_limited, i)
                    dve.tensor_reduce(nmax[:, q1, :], heads(sbank[:, :]), AX.X, ALU.max, negate=True
                                      ).then_inc(s_max, 1)
                if has(3):
                    b3 = (b - 3) % B
                    dve.wait_ge(y_done, i - 2)
                    dve.scalar_tensor_tensor(out=xacc[:, b3, :], in0=ybank[b3 % 2][:, :], scalar=gates[:, 0:1],
                                             in1=xacc[:, b3, :], op0=ALU.mult, op1=ALU.add).then_inc(y_acc, 1)
                if has(1):
                    q1 = (b - 1) % 2
                    dve.wait_ge(s_exp, i)
                    dve.reciprocal(prec[:, q1, :], psums[:, q1, :]).then_inc(s_rec, 1)
                if is_last(g, b) or drain:
                    hb = b - 4 if not drain else b + 4
                    if hb >= 0:
                        h_lo_(hb)
                    hb += 1
                    if hb >= 0:
                        h_norm(hb)

            def h_lo_(hb):
                dve.wait_ge(h_hi, hb + 1)
                subtract_hi(xT[1][:, hb, :, :].rearrange("p c t -> p (c t)"), tbank[:, :],
                            xT[0][:, hb, :, :].rearrange("p c t -> p (c t)"), h_lo)

            def h_norm(hb):
                dve.wait_ge(y_acc, UNITS - B + hb + 1)
                dve.bn_stats(bn[:, 1, hb, :], xacc[:, hb, :]).then_inc(h_step, 1)
                dve.wait_ge(h_step, 2 * hb + 1)
                dve.bn_aggr(mv[:, 1, hb, :], bn[:, 1, hb, :]).then_inc(h_step, 1)
                dve.wait_ge(h_step, 2 * hb + 2)
                dve.tensor_scalar(rstd[:, 1, hb:hb + 1], mv[:, 1, hb, 1:2], LN_EPS, None, ALU.add
                                  ).then_inc(h_var, 1)
                dve.wait_ge(h_rstd, hb + 1)
                if hb >= NROW:
                    dve.wait_ge(h_t, hb - NROW + 1)
                dve.tensor_scalar(rows[:, hb % NROW, :], xacc[:, hb, :], mv[:, 1, hb, 0:1], rstd[:, 1, hb:hb + 1],
                                  ALU.subtract, ALU.mult).then_inc(h_row, 1)
                dve.wait_ge(h_row, hb + 1)
                dve.tensor_reduce(absum[:, hb:hb + 1], rows[:, hb % NROW, :], AX.X, ALU.add,
                                  apply_absolute_value=True).then_inc(h_abs, 1)

            groups(dve, unit)
            h_lo_(B - 1)

            steps = [0]

            def then(ins):
                ins.then_inc(rt, 1)
                steps[0] += 1
                dve.wait_ge(rt, steps[0])

            def tt(o, a, b_, op):
                then(dve.tensor_tensor(o, a, b_, op))

            def ts(o, a, s1, s2, op0, op1=ALU.bypass):
                then(dve.tensor_scalar(o, a, s1, s2, op0, op1) if s2 is not None
                     else dve.tensor_scalar(o, a, s1, None, op0))

            def over_e(ap):
                return ap.unsqueeze(2).to_broadcast([P, B, NX])

            def over_b(ap):
                return ap.unsqueeze(1).to_broadcast([P, B, NX])

            dve.wait_ge(route_mm, 1)
            text, vision, ratio = r8[:, 0, :], r8[:, 1, :], r8[:, 2, :]
            ts(text, sbank[:, 64:64 + B], 1.0 / ((P - VISION) * E), None, ALU.mult)
            ts(vision, sbank[:, 64 + B:64 + 2 * B], 1.0 / (VISION * E), 1e-8, ALU.mult, ALU.add)
            then(dve.reciprocal(ratio, vision))
            tt(ratio, ratio, text, ALU.mult)
            logit = lg[:, 0, :, :]
            tt(lg[:, 2, :, :], over_e(ratio), over_b(gwm[:, 0, :]), ALU.mult)
            tt(lg[:, 3, :, :], lg[:, 2, :, :],
               sbank[:, 0:4 * B].rearrange("p (b e) -> p b e", e=4)[:, :, 0:NX], ALU.add)
            tt(lg[:, 2, :, :], lg[:, 3, :, :], over_b(gwm[:, 1, :]), ALU.add)
            then(dve.tensor_reduce(r8[:, 3, :], lg[:, 2, :, :], AX.X, ALU.max))
            dve.tensor_tensor(logit, lg[:, 2, :, :], over_e(r8[:, 3, :]), ALU.subtract).then_inc(score_exp_in, 1)
            dve.wait_ge(score_exp, 1)
            then(dve.tensor_reduce(r8[:, 4, :], lg[:, 1, :, :], AX.X, ALU.add))
            then(dve.reciprocal(r8[:, 5, :], r8[:, 4, :]))
            score = lg[:, 4, :, :]
            dve.tensor_tensor(score, lg[:, 1, :, :], over_e(r8[:, 5, :]), ALU.mult).then_inc(tok0_in, 1)
            dve.wait_ge(tok0_in, 1)

            def first_max(sc, top, hot, spare):
                then(dve.tensor_reduce(top, sc, AX.X, ALU.max))
                tt(hot, sc, over_e(top), ALU.is_equal)
                ts(spare, hot[:, :, 0], -1.0, 1.0, ALU.mult, ALU.add)
                tt(hot[:, :, 1], hot[:, :, 1], spare, ALU.mult)
                tt(spare, spare, hot[:, :, 1], ALU.subtract)
                tt(hot[:, :, 2], hot[:, :, 2], spare, ALU.mult)

            def second(sc, hot, gone):
                ts(gone, hot, -4.0, None, ALU.mult)
                tt(gone, gone, sc, ALU.add)

            first_max(score, r8[:, 6, :], lg[:, 5, :, :], r8[:, 8, :])
            second(score, lg[:, 5, :, :], lg[:, 6, :, :])
            then(dve.tensor_reduce(r8[:, 7, :], lg[:, 6, :, :], AX.X, ALU.max))
            tt(r8[:, 8, :], r8[:, 6, :], r8[:, 7, :], ALU.add)
            ts(r8[:, 8, :], r8[:, 8, :], 1e-8, None, ALU.add)
            then(dve.reciprocal(r8[:, 9, :], r8[:, 8, :]))
            ts(r8[:, 9, :], r8[:, 9, :], gates[:, 1:2], None, ALU.mult)
            tt(r8[:, 6, :], r8[:, 6, :], r8[:, 9, :], ALU.mult)
            tt(r8[:, 7, :], r8[:, 7, :], r8[:, 9, :], ALU.mult)
            dve.wait_ge(tok0_mm, 1)
            then(dve.tensor_copy(lg[:, 7, :, :].rearrange("p b e -> p (b e)"), sbank[:, 128:128 + B * NX]))
            first_max(lg[:, 7, :, :], r8[:, 10, :], lg[:, 5, :, :], r8[:, 8, :])
            second(lg[:, 7, :, :], lg[:, 5, :, :], lg[:, 8, :, :])
            first_max(lg[:, 8, :, :], r8[:, 10, :], lg[:, 6, :, :], r8[:, 8, :])
            tt(lg[:, 5, :, :], lg[:, 5, :, :], over_e(r8[:, 6, :]), ALU.mult)
            tt(lg[:, 6, :, :], lg[:, 6, :, :], over_e(r8[:, 7, :]), ALU.mult)
            dve.tensor_tensor(coef[:, :, :], lg[:, 5, :, :], lg[:, 6, :, :], ALU.add).then_inc(coef_ok, 1)
            dve.wait_ge(coef_ok, 1)
            dve.wait_ge(b2_in, 16 * NX)

            def activations_lo(s):
                for f in range(EC):
                    l = s * EC + f
                    dve.wait_ge(f_hi, l + 1)
                    subtract_hi(acts(1, s)[:, f, :], prob[:, l % 2, :], acts(0, s)[:, f, :], f_lo)

            def add_expert(s):
                for k in range(4):
                    u, e, b = s * 4 + k, s // 2, (s % 2) * 4 + k
                    if e >= 1:
                        dve.wait_ge(f_acc, (e - 1) * B + b + 1)
                    dve.scalar_tensor_tensor(out=xacc[:, b, :], in0=b2row[e], scalar=coef[:, b, e:e + 1],
                                             in1=xacc[:, b, :], op0=ALU.mult, op1=ALU.add).then_inc(f_bias, 1)
                    dve.wait_ge(f_bias, u + 1)
                    dve.wait_ge(f2, u + 1)
                    dve.scalar_tensor_tensor(out=xacc[:, b, :], in0=ybank[u % 2][:, :], scalar=coef[:, b, e:e + 1],
                                             in1=xacc[:, b, :], op0=ALU.mult, op1=ALU.add).then_inc(f_acc, 1)

            activations_lo(0)
            for s in range(1, 2 * NX):
                activations_lo(s)
                add_expert(s - 1)
            add_expert(2 * NX - 1)


_INS = ["x", "ctx_4096", "pos_BxS2", "mask_BxSxS2_ik0", "g_xattn", "g_ffn", "L0_xattn_Wq", "L0_xattn_Wk",
        "L0_xattn_Wv", "L0_xattn_Wo", "L0_ffn_gate_w", "L0_ffn_gate_b", "L0_ffn_w1", "L0_ffn_b1",
        "L0_ffn_w2", "L0_ffn_b2"]


def kernel(**inputs):
    import numpy as np
    import concourse.bacc as bacc
    from concourse.bass_utils import run_bass_kernel_spmd as run

    nc = bacc.Bacc("TRN2", target_bir_lowering=False, num_devices=1)
    arrays, args = {}, []
    for name in _INS:
        a = np.ascontiguousarray(inputs[name])
        arrays[f"in_{name}"] = a
        args.append(nc.dram_tensor(f"in_{name}", a.shape, mybir.dt.from_np(a.dtype), kind="ExternalInput").ap())
    freq = np.float32(1) / np.power(np.float32(10000.0), np.arange(0, D, 2, dtype=np.float32) / np.float32(D))
    angle = np.arange(MAX_POS, dtype=np.float32)[:, None] * freq[None, :]
    table = np.concatenate([np.cos(angle), -np.sin(angle), np.sin(angle)], axis=1)
    arrays["rope_rows"] = table
    rope_rows = nc.dram_tensor("rope_rows", table.shape, F32, kind="ExternalInput").ap()
    kv_scratch = nc.dram_tensor("kv_scratch", (KVH, B, P, 4, P), F32, kind="Internal").ap()
    out = nc.dram_tensor("out", (B, P, E), F32, kind="ExternalOutput").ap()
    build(nc, *args, rope_rows, kv_scratch, out)
    r = run(nc, [arrays], core_ids=[0])
    return r.results[0]["out"]
```

```python
from contextlib import ExitStack

import concourse.bass as bass
from concourse import mybir

ALU = mybir.AluOpType
ACT = mybir.ActivationFunctionType
AX = mybir.AxisListType
F32 = mybir.dt.float32
F32R = mybir.dt.float32r
I32 = mybir.dt.int32

P = 128
B = 8
E = 512
EC = E // P
H, KVH, D = 32, 8, 128
HG = H // KVH
GH = KVH // HG
HALF = D // 2
MAX_POS = 512
NX = 3
VISION = int(P * 0.3)
SCALE = float(D) ** -0.5
MASKED = -1.0e9
LN_EPS = 1e-5
KEEP = 3.0e38
UNITS = KVH * B
NROW = 4
NW = 4
NKV = 4
NST = 3
BH = B // 2
LAG_S, LAG_P, LAG_Y = 5, 6, 7
W_PER = 2 * EC
W_B = 4 * EC
W_C = W_B + KVH * W_PER
W_A = W_B + EC
W_DVE = 2 * EC


def build(nc, x, ctx_in, pos, mask, g_xattn, g_ffn, Wq, Wk, Wv, Wo, gate_w, gate_b, w1, b1, w2, b2,
          rope_rows, kv_scratch, out):
    with ExitStack() as stack:
        def sb(name, shape, dt=F32):
            return stack.enter_context(nc.sbuf_tensor(name, shape, dt))

        def bank(name):
            return stack.enter_context(nc.psum_tensor(name, [P, 512], F32))

        def sem(name):
            return stack.enter_context(nc.semaphore(name))

        xT = [sb(f"xT_{s}", [P, B, EC, P], F32R) for s in ("hi", "lo")]
        cT = [sb(f"cT_{s}", [P, B, EC, P], F32R) for s in ("hi", "lo")]
        wa = [[sb(f"wa{n}_{s}", [P, EC, 512], F32R) for s in ("hi", "lo")] for n in range(2)]
        wb = [[sb(f"wb{n}_{s}", [P, EC, 512], F32R) for s in ("hi", "lo")] for n in range(2)]
        wraw = sb("wraw", [P, NW, 512])
        split = sb("split", [P, NST, 2, 512], F32R)
        kv = sb("kv", [P, NKV, 4, P], F32R)
        xacc = sb("xacc", [P, B, E])
        rows = sb("rows", [P, NROW, E])
        rope = sb("rope", [P, 2, B, P])
        limit = sb("limit", [P, B, P])
        rot = sb("rot", [P, 2, 512])
        roped = sb("roped", [P, 512])
        prob = sb("prob", [P, 2, 512])
        ident = sb("ident", [P, P])
        sel = sb("sel", [P, 3, P])
        posi = sb("posi", [P, B], I32)
        posf = sb("posf", [P, 3, B])
        gates = sb("gates", [P, 2])
        bn = sb("bn", [P, 2, B, 6])
        mv = sb("mv", [P, 2, B, 2])
        nmr = sb("nmr", [P, 2, B])
        rstd = sb("rstd", [P, 2, B])
        mhalf = sb("mhalf", [P, B])
        nmax = sb("nmax", [P, 2, HG])
        psums = sb("psums", [P, 2, HG])
        prec = sb("prec", [P, 2, HG])
        gw = sb("gw", [P, EC, 4])
        gws = [sb(f"gws_{s}", [P, EC, 4], F32R) for s in ("hi", "lo")]
        gwm = sb("gwm", [P, 2, NX])
        b1c = sb("b1c", [P, NX, EC])
        absum = sb("absum", [P, B])
        r8 = sb("r8", [P, 12, B])
        lg = sb("lg", [P, 10, B, NX])
        coef = sb("coef", [P, B, NX])

        qbank = [bank("q0"), bank("q1")]
        tbank = bank("qt")
        sbank = bank("s")
        pbank = bank("pt")
        obank = bank("o")
        ybank = [bank("y0"), bank("y1")]
        trans = [pbank, obank]

        row_in = [sem(f"row_in{k}") for k in range(NROW)]
        x_in = [sem(f"x_in{b}") for b in range(B)]
        small_in = sem("small_in")
        pos_in = sem("pos_in")
        mask_in = sem("mask_in")
        w_in = [sem(f"w_in{k}") for k in range(NW)]
        w_hi, w_lo = sem("w_hi"), sem("w_lo")
        pool_const, ident_ok = sem("pool_const"), sem("ident_ok")
        pos_step, pos_ok = sem("pos_step"), sem("pos_ok")
        rope_in, rope_t, rope_ok = sem("rope_in"), sem("rope_t"), sem("rope_ok")
        lim_step, limit_ok = sem("lim_step"), sem("limit_ok")
        gates_ok = sem("gates_ok")
        ln_step, ln_var, ln_rstd, ln_row = sem("ln_step"), sem("ln_var"), sem("ln_rstd"), sem("ln_row")
        ln_nmr, h_nmr = sem("ln_nmr"), sem("h_nmr")
        row_t, row_hi, row_lo = sem("row_t"), sem("row_hi"), sem("row_lo")
        k_proj, k_rot, k_roped = sem("k_proj"), sem("k_rot"), sem("k_roped")
        v_proj = sem("v_proj")
        u_hi, u_lo = sem("u_hi"), sem("u_lo")
        stored = [sem(f"stored{k}") for k in range(NST)]
        kv_in = [sem(f"kv_in{k}") for k in range(NKV)]
        q_proj, q_rot, q_roped = sem("q_proj"), sem("q_rot"), sem("q_roped")
        q_hi, q_lo = sem("q_hi"), sem("q_lo")
        s_done, s_limited, s_max, s_exp = sem("s_done"), sem("s_limited"), sem("s_max"), sem("s_exp")
        s_rec, p_norm, p_t, p_hi, p_lo = sem("s_rec"), sem("p_norm"), sem("p_t"), sem("p_hi"), sem("p_lo")
        o_done, o_hi, o_lo = sem("o_done"), sem("o_hi"), sem("o_lo")
        y_done, y_acc = sem("y_done"), sem("y_acc")
        h_step, h_var, h_rstd, h_row = sem("h_step"), sem("h_var"), sem("h_rstd"), sem("h_row")
        h_abs = sem("h_abs")
        h_t, h_hi, h_lo = sem("h_t"), sem("h_hi"), sem("h_lo")
        gw_hi, gw_lo = sem("gw_hi"), sem("gw_lo")
        route_mm, score_exp_in, score_exp, tok0_in, tok0_mm = (
            sem("route_mm"), sem("score_exp_in"), sem("score_exp"), sem("tok0_in"), sem("tok0_mm"))
        rt = sem("rt")
        coef_ok = sem("coef_ok")
        f1, f_act, f_hi, f_lo = sem("f1"), sem("f_act"), sem("f_hi"), sem("f_lo")
        f2, f_acc, f_bias = sem("f2"), sem("f_acc"), sem("f_bias")
        b2_in = sem("b2_in")
        out_done = sem("out_done")

        rope4 = rope[:, :, :, :].rearrange("p c b t -> p (c b t)").rearrange("p (k n) -> p k n", n=E)
        b2row = [rope4[:, e, :] for e in range(NX)]
        unread = rope4[:, NX, :]
        rope_rows_sb = [t[:, :, :].rearrange("p a (b n) -> p (a b) n", n=2 * D) for t in (rot, prob)]

        ctx_rows = ctx_in
        w_chunks = []
        for half in range(GH):
            for m in (Wk, Wv):
                w_chunks += [m[c * P:(c + 1) * P, half * 512:(half + 1) * 512] for c in range(EC)]
        assert len(w_chunks) == W_B

        def w_target(n):
            if n < W_B:
                half, kind, c = n // (2 * EC), n // EC % 2, n % EC
                return (wa, wb)[kind][half], c
            kind, c = (n - W_B) // EC % 2, n % EC
            return (wa, wb)[kind][(n - W_B) // W_PER % 2], c

        def heads(ap):
            return ap.rearrange("p (h k) -> p h k", h=HG)

        PASSES = ((0, 0), (0, 1), (1, 0))

        def project(pe, bank_, stationary, moving, chunks=EC):
            for c in range(chunks):
                for n, (s, m) in enumerate(PASSES):
                    mm = pe.matmul(bank_[:, :], stationary(s, c), moving(m, c),
                                   start=(c == 0 and n == 0), stop=(c == chunks - 1 and n == 2))
            return mm

        def project_tile(pe, bank_, weights, h, source, half, between=None):
            for c in range(EC):
                for n, (s, m) in enumerate(PASSES):
                    mm = pe.matmul(bank_[:, :].rearrange("p (b t) -> p b t", b=BH),
                                   weights[s][:, c, h * P:(h + 1) * P],
                                   source[m][:, half * BH:(half + 1) * BH, c, :],
                                   start=(c == 0 and n == 0), stop=(c == EC - 1 and n == 2))
                    if between is not None:
                        between(3 * c + n)
            return mm

        def q_lo_count(j, b, g):
            return j + (BH - (b - LAG_S) % BH)

        def groups(eng, unit):
            for b in range(B):
                unit(0, 0, b, b, False)
            with eng.Fori(1, KVH - 2, 2) as g:
                for par in (1, 0):
                    for b in range(B):
                        unit(g + (1 - par), par, b, B, False)
            for b in range(B):
                unit(KVH - 1, 1, b, B, False)
            for b in range(LAG_Y):
                unit(KVH, 0, b, B, True)

        def lagged(par, b, lag):
            return (par if b >= lag else 1 - par), (b - lag) % B

        def tile_a(m):
            return m % 2 == 0, m // (2 * B), m // 2 % B, m // 2

        def q_split(s, g_half, h):
            flat = cT[s][:, :, :, :].rearrange("p b c t -> p (b c t)")
            at = (g_half % 2 * HG + h) * 512
            return flat[:, at:at + 512]

        def is_last(g, b):
            return isinstance(g, int) and g == KVH - 1

        def acts(a, s):
            return cT[a][:, (s % 2) * 4:(s % 2) * 4 + 4, :, :].rearrange("p b c t -> p b (c t)")

        def bcast(row, n):
            return row.rearrange("(a n) -> a n", a=1).to_broadcast([P, n])

        def store(sp, m):
            keys, half, k, _ = tile_a(m)
            sp.wait_ge(u_lo, m + 1)
            for s in range(2):
                if keys:
                    dst = kv_scratch[half * HG + k % HG, k // HG * BH:(k // HG + 1) * BH, :, s, :]
                else:
                    dst = kv_scratch[half * HG:(half + 1) * HG, k, :, 2 + s, :]
                sp.dma_start(dst.rearrange("g p k -> p g k"),
                             heads(split[:, m % NST, s, :].bitcast(F32))).then_inc(stored[m % NST], 16)

        def expert_chunk(n):
            e, k = (n - W_C) // W_PER, (n - W_C) % W_PER
            return w1[e, k * P:(k + 1) * P, :] if k < EC else w2[e, (k - EC) * P:(k - EC + 1) * P, :]

        block = stack.enter_context(nc.Block())

        @block.sync
        def _(sp):
            def w_load(n, src):
                if n >= NW:
                    sp.wait_ge(w_lo, n - NW + 1)
                return sp.dma_start(wraw[:, n % NW, :], src)

            sp.dma_start(posi[:, :], pos.rearrange("b s -> s b"), allow_slow_non_contiguous=True
                         ).then_inc(pos_in, 16)
            for t in range(NROW):
                sp.dma_start(rows[:, t, :], ctx_rows[t]).then_inc(row_in[t], 16)
                w_load(t, w_chunks[t]).then_inc(w_in[t], 16)
            for n in range(NW, W_DVE):
                w_load(n, w_chunks[n]).then_inc(w_in[n % NW], 16)
            for t in range(NROW, B):
                sp.wait_ge(row_t, t - NROW + 1)
                sp.dma_start(rows[:, t % NROW, :], ctx_rows[t]).then_inc(row_in[t % NROW], 16)

            for m in range(4 * B):
                n = W_DVE + m
                if n < W_A:
                    src = w_chunks[n] if n < W_B else Wq[(n - W_B) * P:(n - W_B + 1) * P, 0:512]
                    w_load(n, src).then_inc(w_in[n % NW], 16)
                if m < B:
                    sp.dma_start(xacc[:, m, :], x[m]).then_inc(x_in[m], 16)
                if m == B:
                    sp.dma_start(limit[:, :, :].bitcast(I32), mask.rearrange("b q k -> q b k")).then_inc(mask_in, 16)
                    sp.dma_start(gates[:, 0:1], bcast(g_xattn, 1)).then_inc(small_in, 16)
                    sp.dma_start(gates[:, 1:2], bcast(g_ffn, 1)).then_inc(small_in, 16)
                    sp.dma_start(gwm[:, 0, :], bcast(gate_w[E, :], NX)).then_inc(small_in, 16)
                    sp.dma_start(gwm[:, 1, :], bcast(gate_b, NX)).then_inc(small_in, 16)
                    sp.wait_ge(pool_const, 1)
                    sp.dma_start(gw[:, :, 0:NX], gate_w[0:E, :].rearrange("(c p) e -> p c e", p=P),
                                 allow_slow_non_contiguous=True).then_inc(small_in, 16)
                    for e in range(NX):
                        sp.dma_start(b1c[:, e, :], b1[e].rearrange("(c p) -> p c", p=P),
                                     allow_slow_non_contiguous=True).then_inc(small_in, 16)
                if m >= 1:
                    store(sp, m - 1)
            store(sp, 4 * B - 1)

            def unit(g, par, b, past, drain):
                i = g * B + b
                if not drain:
                    n = g * W_PER + (W_A + b)
                    sp.wait_ge(w_lo, n - NW + 1)
                    if b < EC:
                        src = Wo[bass.ds(g * 512 + b * P, P), :]
                    elif is_last(g, b):
                        src = w1[0, (b - EC) * P:(b - EC + 1) * P, :]
                    else:
                        src = Wq[(b - EC) * P:(b - EC + 1) * P, bass.ds(g * 512 + 512, 512)]
                    sp.dma_start(wraw[:, b % NW, :], src).then_inc(w_in[b % NW], 16)
                else:
                    n = W_A + KVH * W_PER + b
                    w_load(n, expert_chunk(n)).then_inc(w_in[n % NW], 16)
                if past == 0:
                    for k in range(NST):
                        sp.wait_ge(stored[k], 32 * len(range(k, 4 * B, NST)))
                if past >= LAG_S and (not drain or b < LAG_S):
                    pj, bj = lagged(par, b, LAG_S)
                    gj = g if b >= LAG_S else g - 1
                    if past - LAG_S >= NKV or past == B:
                        if not (isinstance(g, int) and i - LAG_S < NKV):
                            sp.wait_ge(o_done, i - LAG_S - NKV + 1)
                    sp.dma_start(kv[:, bj % NKV, :, :].bitcast(F32), kv_scratch[gj, bj]
                                 ).then_inc(kv_in[bj % NKV], 16)

            groups(sp, unit)

            sp.wait_ge(q_rot, UNITS)
            for e in range(NX):
                sp.dma_start(b2row[e], bcast(b2[e], E)).then_inc(b2_in, 16)
            for n in range(W_A + KVH * W_PER + LAG_Y, W_C + NX * W_PER):
                w_load(n, expert_chunk(n)).then_inc(w_in[n % NW], 16)
            for b in range(B):
                sp.wait_ge(f_acc, (NX - 1) * B + b + 1)
                sp.dma_start(out[b], xacc[:, b, :]).then_inc(out_done, 16)
            sp.wait_ge(out_done, 16 * B)

        @block.tensor
        def _(pe):
            def transpose4(bank_, src, done):
                for c in range(4):
                    mm = pe.transpose(bank_[:, c * P:(c + 1) * P], src(c), ident[:, :])
                mm.then_inc(done, 1)

            def row_transpose(t):
                if t < B:
                    pe.wait_ge(row_in[t % NROW], 16 * (t // NROW + 1))
                else:
                    pe.wait_ge(ln_row, t - B + 1)
                if t >= 2:
                    pe.wait_ge(row_lo, t - 1)
                transpose4(trans[t % 2], lambda c: rows[:, t % NROW, c * P:(c + 1) * P], row_t)

            def rope_transpose(k):
                pe.wait_ge(rope_in, 16 * B)
                if k >= 1:
                    pe.wait_ge(rope_ok, k)
                src = rope_rows_sb[k // 2]
                transpose4(tbank, lambda c: src[:, 2 * (k % 2) + c // 2, c % 2 * P:(c % 2 + 1) * P], rope_t)

            pe.wait_ge(ident_ok, 2)
            for t in range(BH):
                row_transpose(t)
            for m in range(4 * B):
                keys, half, k, n = tile_a(m)
                if m == 0:
                    pe.wait_ge(row_lo, BH)
                elif keys and k == HG and half == 0:
                    pe.wait_ge(row_lo, B)
                if k == 0:
                    pe.wait_ge(w_lo, (2 * half + (not keys) + 1) * EC)
                if keys:
                    if n >= 2:
                        pe.wait_ge(k_rot, n - 1)
                    project_tile(pe, qbank[n % 2], wa[half], k % HG, cT, k // HG).then_inc(k_proj, 1)
                else:
                    if n >= 2:
                        pe.wait_ge(u_lo, m - 3)
                    project(pe, ybank[n % 2], lambda s, c: cT[s][:, k, c, :],
                            lambda s, c: wb[half][s][:, c, :]).then_inc(v_proj, 1)
                if m in (0, 2, 4, 6):
                    if m == 0:
                        rope_transpose(0)
                        rope_transpose(1)
                    if m == 2:
                        rope_transpose(2)
                        rope_transpose(3)
                    row_transpose(BH + m // 2)
                if m >= 2 * B and keys:
                    row_transpose(B + (m - 2 * B) // 2)

            def unit(g, par, b, past, drain):
                i = g * B + b

                def has(lag):
                    return past >= lag and (not drain or b < lag)

                def score_products(k):
                    h, (s, m) = k // 3, PASSES[k % 3]
                    _, bs = lagged(par, b, LAG_S)
                    q = q_split(s, bs // BH, h)
                    mm = pe.matmul(sbank[:, h * P:(h + 1) * P], q[:, bs % BH * P:(bs % BH + 1) * P],
                                   kv[:, bs % NKV, m, :], start=(k % 3 == 0), stop=(k % 3 == 2))
                    if k == 3 * HG - 1:
                        mm.then_inc(s_done, 1)

                if drain and b >= 1:
                    h_transpose(b - 1)
                if has(0):
                    if b == 0:
                        pe.wait_ge(w_lo, g * W_PER + (W_B + EC))
                    if past == 0:
                        pe.wait_ge(row_lo, B + BH)
                    if past == BH:
                        pe.wait_ge(row_lo, 2 * B)
                    if past >= 2:
                        pe.wait_ge(q_rot, i - 1)
                    else:
                        pe.wait_ge(k_rot, 2 * B)
                if has(LAG_S):
                    pe.wait_ge(q_lo, q_lo_count(i - LAG_S, b, g))
                    _, bs = lagged(par, b, LAG_S)
                    pe.wait_ge(kv_in[bs % NKV], (g * 2 + ((b - LAG_S) // NKV + 1)) * 16)
                    if past >= LAG_S + 1:
                        pe.wait_ge(s_exp, i - LAG_S)
                if has(0):
                    mm = project_tile(pe, qbank[b % 2], wa[par], b % HG, xT, b // BH,
                                      score_products if has(LAG_S) else None)
                    mm.then_inc(q_proj, 1)
                elif has(LAG_S):
                    for k in range(3 * HG):
                        score_products(k)
                if has(LAG_P):
                    pe.wait_ge(p_norm, i - LAG_P + 1)
                    if past >= LAG_P + 1:
                        pe.wait_ge(p_lo, i - LAG_P)
                    transpose4(pbank, lambda c: prob[:, 1, c * P:(c + 1) * P], p_t)
                if drain and b >= LAG_S:
                    first_layer(0, b - LAG_S)
                if has(LAG_Y):
                    p3, b3 = lagged(par, b, LAG_Y)
                    pe.wait_ge(o_lo, i - LAG_Y + 1)
                    if b3 == 0:
                        pe.wait_ge(w_lo, g * W_PER + (W_B + W_PER))
                    if not (isinstance(g, int) and i - LAG_Y < 2):
                        pe.wait_ge(y_acc, i - LAG_Y - 1)
                    project(pe, ybank[b3 % 2], lambda s, c: split[:, 2, s, c * P:(c + 1) * P],
                            lambda s, c: wb[p3][s][:, c, :]).then_inc(y_done, 1)
                if has(LAG_P):
                    _, b2_ = lagged(par, b, LAG_P)
                    pe.wait_ge(p_lo, i - LAG_P + 1)
                    if past >= LAG_P + 1:
                        pe.wait_ge(o_lo, i - LAG_P)
                    for n, (s, m) in enumerate(PASSES):
                        mm = pe.matmul(obank[:, :], kv[:, b2_ % NKV, 2 + s, :], split[:, 1, m, :],
                                       start=(n == 0), stop=(n == 2))
                    mm.then_inc(o_done, 1)

            def h_transpose(hb):
                pe.wait_ge(h_row, hb + 1)
                if hb >= 1:
                    pe.wait_ge(h_lo, hb)
                transpose4(tbank, lambda c: rows[:, hb % NROW, c * P:(c + 1) * P], h_t)

            def first_layer(s, f):
                e, hf, l = s // 2, s % 2, s * EC + f
                if hf == 0 and f == 0:
                    pe.wait_ge(w_lo, W_C + e * W_PER + EC)
                if l == 0:
                    pe.wait_ge(h_lo, BH)
                if l == EC:
                    pe.wait_ge(h_lo, B)
                if l < 2:
                    pe.wait_ge(q_rot, UNITS)
                else:
                    pe.wait_ge(f_act, l - 1)
                project_tile(pe, qbank[l % 2], wa[e % 2], f, xT, hf).then_inc(f1, 1)

            groups(pe, unit)

            def second_layer(s):
                e, hf = s // 2, s % 2
                if hf == 0:
                    pe.wait_ge(w_lo, W_C + (e + 1) * W_PER)
                pe.wait_ge(f_lo, (s + 1) * EC)
                for k in range(4):
                    u = s * 4 + k
                    if u < 2:
                        pe.wait_ge(y_acc, UNITS - 1 + u)
                    else:
                        pe.wait_ge(f_acc, u - 1)
                    project(pe, ybank[u % 2],
                            lambda a, c: acts(a, s)[:, c, k * P:(k + 1) * P],
                            lambda a, c: wb[e % 2][a][:, c, :]).then_inc(f2, 1)

            def router():
                pe.wait_ge(gw_lo, 1)
                pe.wait_ge(h_abs, B)
                for b in range(B):
                    for c in range(EC):
                        for n, (a, m) in enumerate(PASSES):
                            pe.matmul(sbank[:, 4 * b:4 * b + 4], xT[a][:, b, c, :], gws[m][:, c, :],
                                      start=(c == 0 and n == 0), stop=(c == EC - 1 and n == 2))
                for k in range(2):
                    mm = pe.matmul(sbank[:, 64 + B * k:64 + B * (k + 1)], sel[:, k, :], absum[:, :],
                                   start=True, stop=True)
                mm.then_inc(route_mm, 1)

            def token0():
                pe.wait_ge(tok0_in, 1)
                pe.matmul(sbank[:, 128:128 + B * NX], sel[:, 2, :], lg[:, 4, :, :].rearrange("p b e -> p (b e)"),
                          start=True, stop=True).then_inc(tok0_mm, 1)

            h_transpose(B - 2)
            first_layer(0, 2)
            first_layer(0, 3)
            h_transpose(B - 1)
            for f in range(EC):
                first_layer(1, f)
                if f == 0:
                    router()
                if f == 2:
                    token0()
            for s in range(2, 2 * NX):
                second_layer(s - 2)
                for f in range(EC):
                    first_layer(s, f)
            second_layer(2 * NX - 2)
            second_layer(2 * NX - 1)

        @block.scalar
        def _(act):
            def w_split_hi(n, k, dst):
                act.wait_ge(w_in[k], (n // NW + 1) * 16)
                act.activation(dst, wraw[:, k, :], ACT.Copy).then_inc(w_hi, 1)

            def norm_row(which, b):
                if which == 0:
                    act.wait_ge(ln_nmr, 1)
                    act.wait_ge(row_t, B + b - NROW + 1)
                else:
                    act.wait_ge(h_nmr, b + 1)
                    if b >= NROW:
                        act.wait_ge(h_t, b - NROW + 1)
                    else:
                        act.wait_ge(row_t, 2 * B)
                act.activation(rows[:, b % NROW, :], xacc[:, b, :], ACT.Identity, bias=nmr[:, which, b:b + 1],
                               scale=rstd[:, which, b:b + 1]).then_inc((ln_row, h_row)[which], 1)

            def row_hi_(t):
                act.wait_ge(row_t, t + 1)
                dst = (cT if t < B else xT)[0][:, t % B, :, :]
                act.activation(dst.rearrange("p c t -> p (c t)"), trans[t % 2][:, :], ACT.Copy).then_inc(row_hi, 1)

            def tile_hi(m):
                keys, half, k, n = tile_a(m)
                if m >= NST:
                    act.wait_ge(stored[m % NST], 32 * (m // NST))
                if keys:
                    act.wait_ge(k_roped, n + 1)
                    act.activation(split[:, m % NST, 0, :], roped[:, :], ACT.Copy, scale=SCALE).then_inc(u_hi, 1)
                else:
                    act.wait_ge(v_proj, n + 1)
                    act.activation(split[:, m % NST, 0, :], ybank[n % 2][:, :], ACT.Copy).then_inc(u_hi, 1)

            def rope_copy(k):
                act.wait_ge(rope_t, k + 1)
                act.activation(rope[:, :, 2 * k:2 * k + 2, :],
                               tbank[:, :].rearrange("p (b c t) -> p c b t", b=2, c=2), ACT.Copy
                               ).then_inc(rope_ok, 1)

            def w_hi_to(n):
                buf, c = w_target(n)
                w_split_hi(n, n % NW, buf[0][:, c, :])

            for n in range(EC):
                w_hi_to(n)
                row_hi_(n)
            for n in range(EC, W_DVE):
                w_hi_to(n)
            for k in range(2):
                rope_copy(k)
            for m in range(4 * B):
                if m in (0, 2, 4, 6):
                    if m == 2:
                        rope_copy(2)
                        rope_copy(3)
                    row_hi_(BH + m // 2)
                if m < EC or EC <= m < 2 * EC:
                    w_hi_to(W_DVE + m)
                if 2 * B <= m < 2 * B + EC:
                    if m == 2 * B:
                        act.wait_ge(k_proj, B)
                    w_hi_to(W_B + m - 2 * B)
                if m >= 2 * B and m % 2 == 0:
                    row_hi_(B + (m - 2 * B) // 2)
                if m % 2 == 1:
                    tile_hi(m - 1)
                    tile_hi(m)
                if m >= 2 * B - 1 and m % 2 == 1 and m < 4 * B - 1:
                    norm_row(0, (m - 2 * B + 1) // 2)
            act.wait_ge(small_in, 16 * 8)
            act.activation(gates[:, :], gates[:, :], ACT.Tanh).then_inc(gates_ok, 1)
            act.activation(gws[0][:, :, :], gw[:, :, :], ACT.Copy).then_inc(gw_hi, 1)

            for k in range(NST):
                act.wait_ge(stored[k], 32 * len(range(k, 4 * B, NST)))

            def unit(g, par, b, past, drain):
                i = g * B + b

                def has(lag):
                    return past >= lag and (not drain or b < lag)

                if has(LAG_Y):
                    act.wait_ge(o_done, i - LAG_Y + 1)
                    if not (isinstance(g, int) and i - LAG_Y < 1):
                        act.wait_ge(y_done, i - LAG_Y)
                    act.activation(split[:, 2, 0, :], obank[:, :], ACT.Copy).then_inc(o_hi, 1)
                if not drain:
                    if b == 0 and past >= B:
                        act.wait_ge(y_done, g * B - B)
                    if b == EC:
                        if past >= B:
                            act.wait_ge(q_proj, g * B)
                        else:
                            act.wait_ge(k_proj, 2 * B)
                    buf = wb[par] if b < EC else wa[1 - par]
                    act.wait_ge(w_in[b % NW], (g * 2 + ((W_A + b) // NW + 1)) * 16)
                    act.activation(buf[0][:, b % EC, :], wraw[:, b % NW, :], ACT.Copy).then_inc(w_hi, 1)
                else:
                    if b == EC:
                        act.wait_ge(q_proj, UNITS)
                    w_expert_hi(W_A + KVH * W_PER + b)
                if has(LAG_P):
                    act.wait_ge(p_t, i - LAG_P + 1)
                    if past >= LAG_P + 1:
                        act.wait_ge(o_done, i - LAG_P)
                    act.activation(split[:, 1, 0, :], pbank[:, :], ACT.Copy).then_inc(p_hi, 1)
                if has(1):
                    _, bq = lagged(par, b, 1)
                    act.wait_ge(q_roped, i)
                    if past >= B:
                        act.wait_ge(s_done, s_done_before(i - 1, bq))
                    act.activation(q_split(0, bq // BH, bq % HG), roped[:, :], ACT.Copy).then_inc(q_hi, 1)
                if drain and b >= 1:
                    h_hi_(b - 1)
                if has(LAG_S):
                    act.wait_ge(s_max, i - LAG_S + 1)
                    if past >= LAG_S + 1:
                        act.wait_ge(p_norm, i - LAG_S)
                    q1 = (b - LAG_S) % 2
                    for h in range(HG):
                        a = act.activation(prob[:, 0, h * P:(h + 1) * P], sbank[:, h * P:(h + 1) * P], ACT.Exp,
                                           bias=nmax[:, q1, h:h + 1], accum_out=psums[:, q1, h:h + 1])
                    a.then_inc(s_exp, 1)
                if drain:
                    norm_h(b)
                    if b >= LAG_S:
                        activation_chunk(0, b - LAG_S)

            def s_done_before(t, bq):
                return t - bq % BH - BH

            def w_expert_hi(n):
                e, k = (n - W_C) // W_PER, (n - W_C) % W_PER
                w_split_hi(n, n % NW, (wa if k < EC else wb)[e % 2][0][:, k % EC, :])

            def norm_h(hb):
                norm_row(1, hb)
                act.wait_ge(h_row, hb + 1)
                act.activation(unread, rows[:, hb % NROW, :], ACT.Abs, accum_out=absum[:, hb:hb + 1]
                               ).then_inc(h_abs, 1)

            def h_hi_(hb):
                act.wait_ge(h_t, hb + 1)
                act.activation(xT[0][:, hb, :, :].rearrange("p c t -> p (c t)"), tbank[:, :], ACT.Copy
                               ).then_inc(h_hi, 1)

            def activation_chunk(s, f):
                l, e = s * EC + f, s // 2
                act.wait_ge(f1, l + 1)
                if l < 2:
                    act.wait_ge(p_t, UNITS)
                else:
                    act.wait_ge(f_lo, l - 1)
                func = (ACT.Tanh, ACT.Gelu, ACT.Silu)[e]
                act.activation(prob[:, l % 2, :], qbank[l % 2][:, :], func, bias=b1c[:, e, f:f + 1]
                               ).then_inc(f_act, 1)
                act.wait_ge(f_act, l + 1)
                if s >= 2 and f == 0:
                    act.wait_ge(f2, (s - 1) * 4)
                act.activation(acts(0, s)[:, f, :], prob[:, l % 2, :], ACT.Copy).then_inc(f_hi, 1)

            groups(act, unit)

            n = W_A + KVH * W_PER + LAG_Y
            w_expert_hi(n)
            h_hi_(B - 2)
            activation_chunk(0, 2)
            norm_h(B - 1)
            activation_chunk(0, 3)
            h_hi_(B - 1)
            for l in range(EC, 2 * NX * EC):
                s, f = l // EC, l % EC
                if s >= 1:
                    activation_chunk(s, f)
                if s == 1 and f == 0:
                    act.wait_ge(score_exp_in, 1)
                    act.activation(lg[:, 1, :, :], lg[:, 0, :, :], ACT.Exp).then_inc(score_exp, 1)
                n += 1
                if n < W_C + NX * W_PER:
                    if n == W_C + W_PER + EC:
                        act.wait_ge(y_done, UNITS)
                    if n == W_C + 2 * W_PER:
                        act.wait_ge(f1, 2 * EC)
                    if n == W_C + 2 * W_PER + EC:
                        act.wait_ge(f2, B)
                    w_expert_hi(n)

        @block.gpsimd
        def _(pool):
            pool.memset(gw[:, :, :], 0.0).then_inc(pool_const, 1)
            pool.memset(ident[:, :], 0.0).then_inc(ident_ok, 1)
            pool.wait_ge(ident_ok, 1)
            pool.affine_select(out=ident[:, :], in_=ident[:, :], compare_op=ALU.not_equal, fill=1.0, base=0,
                               pattern=[[-1, P]], channel_multiplier=1).then_inc(ident_ok, 1)
            pool.memset(mhalf[:, :], -0.5).then_inc(pool_const, 1)
            pool.memset(sel[:, :, :], 1.0).then_inc(pool_const, 1)
            pool.wait_ge(pool_const, 3)
            pool.affine_select(out=sel[:, 0, :], in_=sel[:, 0, :], compare_op=ALU.is_ge, fill=0.0, base=-VISION,
                               pattern=[[0, P]], channel_multiplier=1).then_inc(pool_const, 1)
            pool.affine_select(out=sel[:, 1, :], in_=sel[:, 1, :], compare_op=ALU.is_gt, fill=0.0, base=VISION,
                               pattern=[[0, P]], channel_multiplier=-1).then_inc(pool_const, 1)
            pool.affine_select(out=sel[:, 2, :], in_=sel[:, 2, :], compare_op=ALU.is_gt, fill=0.0, base=1,
                               pattern=[[0, P]], channel_multiplier=-1).then_inc(pool_const, 1)

            pool.wait_ge(pos_ok, 1)
            for b in range(B):
                pool.indirect_dma_start(rope_rows_sb[b // BH][:, b % BH, :], None, rope_rows[:, :],
                                        bass.IndirectOffsetOnAxis(ap=posi[:, b:b + 1], axis=0)
                                        ).then_inc(rope_in, 16)

            def w_split_lo(n, buf, c):
                pool.wait_ge(w_hi, n + 1)
                pool.tensor_tensor(buf[1][:, c, :], wraw[:, n % NW, :], buf[0][:, c, :].bitcast(F32), ALU.subtract
                                   ).then_inc(w_lo, 1)

            def w_expert_lo(n):
                e, k = (n - W_C) // W_PER, (n - W_C) % W_PER
                w_split_lo(n, (wa if k < EC else wb)[e % 2], k % EC)

            pool.wait_ge(w_lo, W_DVE)
            for m in range(4 * B):
                keys, half, k, n = tile_a(m)
                if keys:
                    pool.wait_ge(k_rot, n + 1)
                    if n >= 1:
                        pool.wait_ge(u_lo, m - 1)
                    pool.tensor_tensor(roped[:, :], rot[:, 0, :], rot[:, 1, :], ALU.add).then_inc(k_roped, 1)
                if m < 2 * EC:
                    w_split_lo(W_DVE + m, *w_target(W_DVE + m))
                if 2 * B <= m < 2 * B + EC:
                    w_split_lo(W_B + m - 2 * B, *w_target(W_B + m - 2 * B))
                if m == 2 * B - 2:
                    pool.wait_ge(ln_var, 1)
                    pool.tensor_tensor(rstd[:, 0, :], rstd[:, 0, :], mhalf[:, :], ALU.pow).then_inc(ln_rstd, 1)

            pool.wait_ge(u_lo, 4 * B)

            def unit(g, par, b, past, drain):
                i = g * B + b

                def has(lag):
                    return past >= lag and (not drain or b < lag)

                if not drain:
                    buf = wb[par] if b < EC else wa[1 - par]
                    pool.wait_ge(w_hi, g * W_PER + (W_A + b + 1))
                    pool.tensor_tensor(buf[1][:, b % EC, :], wraw[:, b % NW, :],
                                       buf[0][:, b % EC, :].bitcast(F32), ALU.subtract).then_inc(w_lo, 1)
                else:
                    pool.wait_ge(h_var, b + 1)
                    pool.tensor_tensor(rstd[:, 1, b:b + 1], rstd[:, 1, b:b + 1], mhalf[:, 0:1], ALU.pow
                                       ).then_inc(h_rstd, 1)
                    w_expert_lo(W_A + KVH * W_PER + b)
                if has(1):
                    _, bq = lagged(par, b, 1)
                    pool.wait_ge(q_rot, i)
                    if past >= 2:
                        pool.wait_ge(q_lo, i - 1)
                    pool.tensor_tensor(roped[:, :], rot[:, 0, :], rot[:, 1, :], ALU.add).then_inc(q_roped, 1)
                    pool.wait_ge(q_hi, i)
                    pool.tensor_tensor(q_split(1, bq // BH, bq % HG), roped[:, :],
                                       q_split(0, bq // BH, bq % HG).bitcast(F32), ALU.subtract).then_inc(q_lo, 1)
                if has(LAG_S):
                    q1 = (b - LAG_S) % 2
                    pool.wait_ge(s_rec, i - LAG_S + 1)
                    if past >= LAG_S + 1:
                        pool.wait_ge(p_t, i - LAG_S)
                    pool.tensor_tensor(heads(prob[:, 1, :]), heads(prob[:, 0, :]),
                                       prec[:, q1, :].unsqueeze(2).to_broadcast([P, HG, P]), ALU.mult
                                       ).then_inc(p_norm, 1)
                if drain and b >= LAG_S:
                    activation_lo(b - LAG_S)

            def activation_lo(l):
                s, f = l // EC, l % EC
                pool.wait_ge(f_hi, l + 1)
                pool.tensor_tensor(acts(1, s)[:, f, :], prob[:, l % 2, :], acts(0, s)[:, f, :].bitcast(F32),
                                   ALU.subtract).then_inc(f_lo, 1)

            groups(pool, unit)

            n = W_A + KVH * W_PER + LAG_Y
            w_expert_lo(n)
            activation_lo(2)
            pool.wait_ge(h_var, B)
            pool.tensor_tensor(rstd[:, 1, B - 1:B], rstd[:, 1, B - 1:B], mhalf[:, 0:1], ALU.pow).then_inc(h_rstd, 1)
            activation_lo(3)
            for l in range(EC, 2 * NX * EC):
                activation_lo(l)
                n += 1
                if n < W_C + NX * W_PER:
                    w_expert_lo(n)

        @block.vector
        def _(dve):
            def subtract_hi(dst, src, hi, done):
                dve.tensor_tensor(dst, src, hi.bitcast(F32), ALU.subtract).then_inc(done, 1)

            def row_lo_(t):
                dve.wait_ge(row_hi, t + 1)
                T = cT if t < B else xT
                subtract_hi(T[1][:, t % B, :, :].rearrange("p c t -> p (c t)"), trans[t % 2][:, :],
                            T[0][:, t % B, :, :].rearrange("p c t -> p (c t)"), row_lo)

            def tile_lo(m):
                keys, half, k, n = tile_a(m)
                dve.wait_ge(u_hi, m + 1)
                hi, lo = split[:, m % NST, 0, :], split[:, m % NST, 1, :]
                if keys:
                    dve.scalar_tensor_tensor(out=lo, in0=roped[:, :], scalar=SCALE, in1=hi.bitcast(F32),
                                             op0=ALU.mult, op1=ALU.subtract).then_inc(u_lo, 1)
                else:
                    subtract_hi(lo, ybank[n % 2][:, :], hi, u_lo)

            def rotate(bank_, half, done):
                def table(k, a, z):
                    return rope[a:z, k, half * BH:(half + 1) * BH, :].rearrange("p b t -> p (b t)")

                dve.tensor_tensor(rot[:, 0, :], bank_[:, :], table(0, 0, D), ALU.mult)
                dve.tensor_tensor(rot[0:HALF, 1, :], bank_[HALF:D, :], table(1, HALF, D), ALU.mult)
                dve.tensor_tensor(rot[HALF:D, 1, :], bank_[0:HALF, :], table(1, 0, HALF), ALU.mult
                                  ).then_inc(done, 1)

            dve.wait_ge(pos_in, 16)
            dve.tensor_copy(posf[:, 0, :], posi[:, :]).then_inc(pos_step, 1)
            dve.wait_ge(pos_step, 1)
            dve.tensor_scalar(posf[:, 1, :], posf[:, 0, :], 0.0, float(MAX_POS), ALU.is_lt, ALU.mult
                              ).then_inc(pos_step, 1)
            dve.wait_ge(pos_step, 2)
            dve.tensor_tensor(posf[:, 2, :], posf[:, 0, :], posf[:, 1, :], ALU.add).then_inc(pos_step, 1)
            dve.wait_ge(pos_step, 3)
            dve.tensor_scalar(posi[:, :], posf[:, 2, :], 0.0, float(MAX_POS - 1), ALU.max, ALU.min
                              ).then_inc(pos_ok, 1)

            for n in range(W_DVE):
                if n < BH:
                    row_lo_(n)
                buf, c = w_target(n)
                dve.wait_ge(w_hi, n + 1)
                subtract_hi(buf[1][:, c, :], wraw[:, n % NW, :], buf[0][:, c, :], w_lo)
            for m in range(4 * B):
                keys, half, k, n = tile_a(m)
                if m in (0, 2, 4, 6):
                    row_lo_(BH + m // 2)
                if m >= 2 * B and m % 2 == 0:
                    row_lo_(B + (m - 2 * B) // 2)
                if keys:
                    if n == 0:
                        dve.wait_ge(rope_ok, 2)
                    if n == HG:
                        dve.wait_ge(rope_ok, 4)
                    if n == 0:
                        dve.wait_ge(rope_t, 2)
                    else:
                        dve.wait_ge(k_roped, n)
                    dve.wait_ge(k_proj, n + 1)
                    rotate(qbank[n % 2], k // HG, k_rot)
                else:
                    tile_lo(m - 1)
                    if m < 2 * B - 2:
                        for t in ((m - 1) // 2, B - 1)[:2 if m == 2 * B - 3 else 1]:
                            dve.wait_ge(x_in[t], 16)
                            dve.bn_stats(bn[:, 0, t, :], xacc[:, t, :]).then_inc(ln_step, 1)
                            dve.wait_ge(ln_step, 2 * t + 1)
                            dve.bn_aggr(mv[:, 0, t, :], bn[:, 0, t, :]).then_inc(ln_step, 1)
                    tile_lo(m)
                    if m == 2 * B - 3:
                        dve.wait_ge(ln_step, 2 * B)
                        dve.tensor_scalar(rstd[:, 0, :], mv[:, 0, :, 1], LN_EPS, None, ALU.add).then_inc(ln_var, 1)
                    if m == 2 * B - 1:
                        dve.wait_ge(ln_rstd, 1)
                        dve.scalar_tensor_tensor(out=nmr[:, 0, :], in0=mv[:, 0, :, 0], scalar=-1.0,
                                                 in1=rstd[:, 0, :], op0=ALU.mult, op1=ALU.mult).then_inc(ln_nmr, 1)
                if m == 2 * B + 1:
                    keep = prob[:, :, :].rearrange("p t (b k) -> p (t b) k", b=HG)
                    raw = limit[:, :, :].bitcast(I32)
                    dve.wait_ge(mask_in, 16)
                    dve.tensor_scalar(keep, raw, 0.0, KEEP, ALU.not_equal, ALU.mult).then_inc(lim_step, 1)
                    dve.wait_ge(lim_step, 1)
                    dve.tensor_scalar(limit[:, :, :], raw, 0.0, MASKED, ALU.is_equal, ALU.mult).then_inc(lim_step, 1)
                    dve.wait_ge(lim_step, 2)
                    dve.tensor_tensor(limit[:, :, :], limit[:, :, :], keep, ALU.add).then_inc(limit_ok, 1)
            dve.wait_ge(gw_hi, 1)
            subtract_hi(gws[1][:, :, :], gw[:, :, :], gws[0][:, :, :], gw_lo)
            dve.wait_ge(gates_ok, 1)
            dve.wait_ge(limit_ok, 1)
            for k in range(NST):
                dve.wait_ge(stored[k], 32 * len(range(k, 4 * B, NST)))
            dve.wait_ge(k_roped, 2 * B)

            def unit(g, par, b, past, drain):
                i = g * B + b

                def has(lag):
                    return past >= lag and (not drain or b < lag)

                if has(LAG_Y):
                    dve.wait_ge(o_hi, i - LAG_Y + 1)
                    subtract_hi(split[:, 2, 1, :], obank[:, :], split[:, 2, 0, :], o_lo)
                if drain:
                    h_stats(b)
                if has(1):
                    _, bq = lagged(par, b, 1)
                    dve.wait_ge(q_proj, i)
                    if past >= 2:
                        dve.wait_ge(q_roped, i - 1)
                    rotate(qbank[bq % 2], bq // BH, q_rot)
                if has(LAG_S):
                    q1, bs = (b - LAG_S) % 2, (b - LAG_S) % B
                    dve.wait_ge(s_done, i - LAG_S + 1)
                    dve.tensor_tensor(heads(sbank[:, :]), heads(sbank[:, :]),
                                      limit[:, bs, :].unsqueeze(1).to_broadcast([P, HG, P]), ALU.min
                                      ).then_inc(s_limited, 1)
                    dve.wait_ge(s_limited, i - LAG_S + 1)
                    dve.tensor_reduce(nmax[:, q1, :], heads(sbank[:, :]), AX.X, ALU.max, negate=True
                                      ).then_inc(s_max, 1)
                if has(LAG_P):
                    dve.wait_ge(p_hi, i - LAG_P + 1)
                    subtract_hi(split[:, 1, 1, :], pbank[:, :], split[:, 1, 0, :], p_lo)
                if drain and b >= 1:
                    h_lo_(b - 1)
                if has(LAG_S):
                    q1 = (b - LAG_S) % 2
                    dve.wait_ge(s_exp, i - LAG_S + 1)
                    dve.reciprocal(prec[:, q1, :], psums[:, q1, :]).then_inc(s_rec, 1)
                if drain:
                    h_neg_mean(b)
                if has(LAG_Y):
                    b3 = (b - LAG_Y) % B
                    dve.wait_ge(y_done, i - LAG_Y + 1)
                    dve.scalar_tensor_tensor(out=xacc[:, b3, :], in0=ybank[b3 % 2][:, :], scalar=gates[:, 0:1],
                                             in1=xacc[:, b3, :], op0=ALU.mult, op1=ALU.add).then_inc(y_acc, 1)

            def h_lo_(hb):
                dve.wait_ge(h_hi, hb + 1)
                subtract_hi(xT[1][:, hb, :, :].rearrange("p c t -> p (c t)"), tbank[:, :],
                            xT[0][:, hb, :, :].rearrange("p c t -> p (c t)"), h_lo)

            def h_stats(hb):
                dve.wait_ge(y_acc, UNITS - B + hb + 1)
                dve.bn_stats(bn[:, 1, hb, :], xacc[:, hb, :]).then_inc(h_step, 1)
                dve.wait_ge(h_step, 2 * hb + 1)
                dve.bn_aggr(mv[:, 1, hb, :], bn[:, 1, hb, :]).then_inc(h_step, 1)
                dve.wait_ge(h_step, 2 * hb + 2)
                dve.tensor_scalar(rstd[:, 1, hb:hb + 1], mv[:, 1, hb, 1:2], LN_EPS, None, ALU.add
                                  ).then_inc(h_var, 1)

            def h_neg_mean(hb):
                dve.wait_ge(h_rstd, hb + 1)
                dve.scalar_tensor_tensor(out=nmr[:, 1, hb:hb + 1], in0=mv[:, 1, hb, 0:1], scalar=-1.0,
                                         in1=rstd[:, 1, hb:hb + 1], op0=ALU.mult, op1=ALU.mult).then_inc(h_nmr, 1)

            groups(dve, unit)
            h_stats(B - 1)
            h_lo_(B - 2)
            h_neg_mean(B - 1)
            h_lo_(B - 1)

            steps = [0]

            def then(ins):
                ins.then_inc(rt, 1)
                steps[0] += 1
                dve.wait_ge(rt, steps[0])

            def tt(o, a, b_, op):
                then(dve.tensor_tensor(o, a, b_, op))

            def ts(o, a, s1, s2, op0, op1=ALU.bypass):
                then(dve.tensor_scalar(o, a, s1, s2, op0, op1) if s2 is not None
                     else dve.tensor_scalar(o, a, s1, None, op0))

            def over_e(ap):
                return ap.unsqueeze(2).to_broadcast([P, B, NX])

            def over_b(ap):
                return ap.unsqueeze(1).to_broadcast([P, B, NX])

            dve.wait_ge(route_mm, 1)
            text, vision, ratio = r8[:, 0, :], r8[:, 1, :], r8[:, 2, :]
            ts(text, sbank[:, 64:64 + B], 1.0 / ((P - VISION) * E), None, ALU.mult)
            ts(vision, sbank[:, 64 + B:64 + 2 * B], 1.0 / (VISION * E), 1e-8, ALU.mult, ALU.add)
            then(dve.reciprocal(ratio, vision))
            tt(ratio, ratio, text, ALU.mult)
            logit = lg[:, 0, :, :]
            tt(lg[:, 2, :, :], over_e(ratio), over_b(gwm[:, 0, :]), ALU.mult)
            tt(lg[:, 3, :, :], lg[:, 2, :, :],
               sbank[:, 0:4 * B].rearrange("p (b e) -> p b e", e=4)[:, :, 0:NX], ALU.add)
            tt(lg[:, 2, :, :], lg[:, 3, :, :], over_b(gwm[:, 1, :]), ALU.add)
            then(dve.tensor_reduce(r8[:, 3, :], lg[:, 2, :, :], AX.X, ALU.max))
            dve.tensor_tensor(logit, lg[:, 2, :, :], over_e(r8[:, 3, :]), ALU.subtract).then_inc(score_exp_in, 1)
            dve.wait_ge(score_exp, 1)
            then(dve.tensor_reduce(r8[:, 4, :], lg[:, 1, :, :], AX.X, ALU.add))
            then(dve.reciprocal(r8[:, 5, :], r8[:, 4, :]))
            score = lg[:, 4, :, :]
            dve.tensor_tensor(score, lg[:, 1, :, :], over_e(r8[:, 5, :]), ALU.mult).then_inc(tok0_in, 1)
            dve.wait_ge(tok0_in, 1)

            def first_max(sc, top, hot, spare):
                then(dve.tensor_reduce(top, sc, AX.X, ALU.max))
                tt(hot, sc, over_e(top), ALU.is_equal)
                ts(spare, hot[:, :, 0], -1.0, 1.0, ALU.mult, ALU.add)
                tt(hot[:, :, 1], hot[:, :, 1], spare, ALU.mult)
                tt(spare, spare, hot[:, :, 1], ALU.subtract)
                tt(hot[:, :, 2], hot[:, :, 2], spare, ALU.mult)

            def second(sc, hot, gone):
                ts(gone, hot, -4.0, None, ALU.mult)
                tt(gone, gone, sc, ALU.add)

            first_max(score, r8[:, 6, :], lg[:, 5, :, :], r8[:, 8, :])
            second(score, lg[:, 5, :, :], lg[:, 6, :, :])
            then(dve.tensor_reduce(r8[:, 7, :], lg[:, 6, :, :], AX.X, ALU.max))
            tt(r8[:, 8, :], r8[:, 6, :], r8[:, 7, :], ALU.add)
            ts(r8[:, 8, :], r8[:, 8, :], 1e-8, None, ALU.add)
            then(dve.reciprocal(r8[:, 9, :], r8[:, 8, :]))
            ts(r8[:, 9, :], r8[:, 9, :], gates[:, 1:2], None, ALU.mult)
            tt(r8[:, 6, :], r8[:, 6, :], r8[:, 9, :], ALU.mult)
            tt(r8[:, 7, :], r8[:, 7, :], r8[:, 9, :], ALU.mult)
            dve.wait_ge(tok0_mm, 1)
            then(dve.tensor_copy(lg[:, 7, :, :].rearrange("p b e -> p (b e)"), sbank[:, 128:128 + B * NX]))
            first_max(lg[:, 7, :, :], r8[:, 10, :], lg[:, 5, :, :], r8[:, 8, :])
            second(lg[:, 7, :, :], lg[:, 5, :, :], lg[:, 8, :, :])
            first_max(lg[:, 8, :, :], r8[:, 10, :], lg[:, 6, :, :], r8[:, 8, :])
            tt(lg[:, 5, :, :], lg[:, 5, :, :], over_e(r8[:, 6, :]), ALU.mult)
            tt(lg[:, 6, :, :], lg[:, 6, :, :], over_e(r8[:, 7, :]), ALU.mult)
            dve.tensor_tensor(coef[:, :, :], lg[:, 5, :, :], lg[:, 6, :, :], ALU.add).then_inc(coef_ok, 1)
            dve.wait_ge(coef_ok, 1)
            dve.wait_ge(b2_in, 16 * NX)

            def add_expert(s):
                for k in range(4):
                    u, e, b = s * 4 + k, s // 2, (s % 2) * 4 + k
                    if e >= 1:
                        dve.wait_ge(f_acc, (e - 1) * B + b + 1)
                    dve.scalar_tensor_tensor(out=xacc[:, b, :], in0=b2row[e], scalar=coef[:, b, e:e + 1],
                                             in1=xacc[:, b, :], op0=ALU.mult, op1=ALU.add).then_inc(f_bias, 1)
                    dve.wait_ge(f_bias, u + 1)
                    dve.wait_ge(f2, u + 1)
                    dve.scalar_tensor_tensor(out=xacc[:, b, :], in0=ybank[u % 2][:, :], scalar=coef[:, b, e:e + 1],
                                             in1=xacc[:, b, :], op0=ALU.mult, op1=ALU.add).then_inc(f_acc, 1)

            for s in range(2 * NX):
                add_expert(s)


_INS = ["x", "ctx_4096", "pos_BxS2", "mask_BxSxS2_ik0", "g_xattn", "g_ffn", "L0_xattn_Wq", "L0_xattn_Wk",
        "L0_xattn_Wv", "L0_xattn_Wo", "L0_ffn_gate_w", "L0_ffn_gate_b", "L0_ffn_w1", "L0_ffn_b1",
        "L0_ffn_w2", "L0_ffn_b2"]


def kernel(**inputs):
    import numpy as np
    import concourse.bacc as bacc
    from concourse.bass_utils import run_bass_kernel_spmd as run

    nc = bacc.Bacc("TRN2", target_bir_lowering=False, num_devices=1)
    arrays, args = {}, []
    for name in _INS:
        a = np.ascontiguousarray(inputs[name])
        arrays[f"in_{name}"] = a
        args.append(nc.dram_tensor(f"in_{name}", a.shape, mybir.dt.from_np(a.dtype), kind="ExternalInput").ap())
    freq = np.float32(1) / np.power(np.float32(10000.0), np.arange(0, D, 2, dtype=np.float32) / np.float32(D))
    angle = np.arange(MAX_POS, dtype=np.float32)[:, None] * freq[None, :]
    table = np.concatenate([np.cos(angle), np.cos(angle), np.sin(angle), -np.sin(angle)], axis=1)
    arrays["rope_rows"] = table
    rope_rows = nc.dram_tensor("rope_rows", table.shape, F32, kind="ExternalInput").ap()
    kv_scratch = nc.dram_tensor("kv_scratch", (KVH, B, P, 4, P), F32, kind="Internal").ap()
    out = nc.dram_tensor("out", (B, P, E), F32, kind="ExternalOutput").ap()
    build(nc, *args, rope_rows, kv_scratch, out)
    r = run(nc, [arrays], core_ids=[0])
    return r.results[0]["out"]
```

```python
from contextlib import ExitStack

import concourse.bass as bass
from concourse import mybir

ALU = mybir.AluOpType
ACT = mybir.ActivationFunctionType
AX = mybir.AxisListType
F32 = mybir.dt.float32
F32R = mybir.dt.float32r
I32 = mybir.dt.int32

P = 128
B = 8
E = 512
EC = E // P
H, KVH, D = 32, 8, 128
HG = H // KVH
GH = KVH // HG
HALF = D // 2
MAX_POS = 512
NX = 3
VISION = int(P * 0.3)
SCALE = float(D) ** -0.5
MASKED = -1.0e9
LN_EPS = 1e-5
KEEP = 3.0e38
UNITS = KVH * B
NROW = 4
NW = 4
NKV = 4
NST = 3
BH = B // 2
LAG_S, LAG_P, LAG_Y = 5, 6, 7
TILES_A = 4 * B - 2
VALUES_IN = (LAG_S - 2, LAG_S)
VALUES_AT = (LAG_S, LAG_P)
KV_FIRST = 3
FILL = LAG_S
LN_FROM = 5
W_PER = 2 * EC
W_B = 4 * EC
W_C = W_B + KVH * W_PER
W_A = W_B + EC
AHEAD = 2
W_DVE = 2 * EC


def build(nc, x, ctx_in, pos, mask, g_xattn, g_ffn, Wq, Wk, Wv, Wo, gate_w, gate_b, w1, b1, w2, b2,
          rope_rows, kv_scratch, out):
    with ExitStack() as stack:
        def sb(name, shape, dt=F32):
            return stack.enter_context(nc.sbuf_tensor(name, shape, dt))

        def bank(name):
            return stack.enter_context(nc.psum_tensor(name, [P, 512], F32))

        def sem(name):
            return stack.enter_context(nc.semaphore(name))

        xT = [sb(f"xT_{s}", [P, B, EC, P], F32R) for s in ("hi", "lo")]
        cT = [sb(f"cT_{s}", [P, B, EC, P], F32R) for s in ("hi", "lo")]
        wa = [[sb(f"wa{n}_{s}", [P, EC, 512], F32R) for s in ("hi", "lo")] for n in range(2)]
        wb = [[sb(f"wb{n}_{s}", [P, EC, 512], F32R) for s in ("hi", "lo")] for n in range(2)]
        wraw = sb("wraw", [P, NW, 512])
        split = sb("split", [P, NST, 2, 512], F32R)
        kv = sb("kv", [P, NKV, 4, P], F32R)
        xacc = sb("xacc", [P, B, E])
        rows = sb("rows", [P, NROW, E])
        rope = sb("rope", [P, 2, B, P])
        limit = sb("limit", [P, B, P])
        rot = sb("rot", [P, 2, 512])
        roped = sb("roped", [P, 512])
        scores = sb("scores", [P, 512])
        prob = sb("prob", [P, 2, 512])
        ident = sb("ident", [P, P])
        sel = sb("sel", [P, 3, P])
        posi = sb("posi", [P, B], I32)
        posf = sb("posf", [P, 3, B])
        gates = sb("gates", [P, 2])
        bn = sb("bn", [P, 2, B, 6])
        mv = sb("mv", [P, 2, B, 2])
        nmr = sb("nmr", [P, 2, B])
        rstd = sb("rstd", [P, 2, B])
        mhalf = sb("mhalf", [P, B])
        nmax = sb("nmax", [P, 2, HG])
        psums = sb("psums", [P, 2, HG])
        prec = sb("prec", [P, 2, HG])
        gw = sb("gw", [P, EC, 4])
        gws = sb("gws", [P, EC, 2 * 4], F32R)
        fold = sb("fold", [2 * 4, 4])
        gwm = sb("gwm", [P, 2, NX])
        b1c = sb("b1c", [P, NX, EC])
        absum = sb("absum", [P, B])
        coef = sb("coef", [P, B, NX])

        qbank = [bank("q0"), bank("q1")]
        sbanks = stack.enter_context(nc.psum_tensor("s", [P, 1024], F32))
        sbank, tbank = sbanks[:, 0:512], sbanks[:, 512:1024]
        score_parts = sbanks[:, :].rearrange("p (h m k) -> p h m k", h=HG, m=2)
        pbank = bank("pt")
        obank = bank("o")
        ybank = [bank("y0"), bank("y1")]
        rope_bank = [tbank, ybank[1]]
        trans = [pbank, obank]
        trans_first = [pbank, obank, ybank[0], tbank]

        row_in = [sem(f"row_in{k}") for k in range(NROW)]
        x_in = [sem(f"x_in{b}") for b in range(B)]
        small_in = sem("small_in")
        pos_in = sem("pos_in")
        mask_in = sem("mask_in")
        w_in = [sem(f"w_in{k}") for k in range(NW)]
        w_hi, w_lo = sem("w_hi"), sem("w_lo")
        pool_const, ident_ok = sem("pool_const"), sem("ident_ok")
        pos_step, pos_ok = sem("pos_step"), sem("pos_ok")
        rope_in = [sem(f"rope_in{k}") for k in range(2)]
        rope_t, rope_ok = sem("rope_t"), sem("rope_ok")
        lim_step, limit_ok = sem("lim_step"), sem("limit_ok")
        gates_ok = sem("gates_ok")
        ln_step, ln_var, ln_rstd, ln_row = sem("ln_step"), sem("ln_var"), sem("ln_rstd"), sem("ln_row")
        ln_nmr, h_nmr = sem("ln_nmr"), sem("h_nmr")
        row_t, row_hi, row_lo = sem("row_t"), sem("row_hi"), sem("row_lo")
        k_proj, k_rot, k_roped = sem("k_proj"), sem("k_rot"), sem("k_roped")
        v_proj = sem("v_proj")
        u_hi, u_lo = sem("u_hi"), sem("u_lo")
        stored = [sem(f"stored{k}") for k in range(NST)]
        kv_in = [sem(f"kv_in{k}") for k in range(NKV)]
        q_proj, q_rot, q_roped = sem("q_proj"), sem("q_rot"), sem("q_roped")
        q_hi, q_lo = sem("q_hi"), sem("q_lo")
        s_done, s_part, s_sum, s_limited = sem("s_done"), sem("s_part"), sem("s_sum"), sem("s_limited")
        s_max, s_exp = sem("s_max"), sem("s_exp")
        s_rec, p_norm, p_t, p_hi, p_lo = sem("s_rec"), sem("p_norm"), sem("p_t"), sem("p_hi"), sem("p_lo")
        o_done, o_hi, o_lo = sem("o_done"), sem("o_hi"), sem("o_lo")
        y_done, y_acc = sem("y_done"), sem("y_acc")
        h_step, h_var, h_rstd, h_row = sem("h_step"), sem("h_var"), sem("h_rstd"), sem("h_row")
        h_abs = sem("h_abs")
        h_t, h_hi, h_lo = sem("h_t"), sem("h_hi"), sem("h_lo")
        gw_hi, gw_lo = sem("gw_hi"), sem("gw_lo")
        fold_ok, gate_mm, gate_in = sem("fold_ok"), sem("gate_mm"), sem("gate_in")
        route_mm, score_exp_in, score_exp, tok0_in, tok0_mm = (
            sem("route_mm"), sem("score_exp_in"), sem("score_exp"), sem("tok0_in"), sem("tok0_mm"))
        route_step = sem("route_step")
        coef_ok = sem("coef_ok")
        f1, f_act, f_hi, f_lo = sem("f1"), sem("f_act"), sem("f_hi"), sem("f_lo")
        f2, f_acc, f_bias = sem("f2"), sem("f_acc"), sem("f_bias")
        b2_in = sem("b2_in")
        out_done = sem("out_done")

        rope4 = rope[:, :, :, :].rearrange("p c b t -> p (c b t)").rearrange("p (k n) -> p k n", n=E)
        b2row = [rope4[:, e, :] for e in range(NX)]
        unread = rope4[:, NX, :]
        (text, vision, ratio, logit_max, exp_sum, exp_inv, weight1, weight2, spare, pair_inv, top
         ) = [scores[:, n * B:(n + 1) * B] for n in range(11)]
        (logit, exps, part, logit_sum, score, choice1, choice2, score0, score0_rest) = [
            scores[:, n * B * NX:(n + 1) * B * NX].rearrange("p (b e) -> p b e", e=NX) for n in range(4, 13)]
        rope_rows_sb = [t[:, :, :].rearrange("p a (b n) -> p (a b) n", n=2 * D) for t in (rot, prob)]

        w_chunks = []
        for half in range(GH):
            for m in (Wk, Wv):
                w_chunks += [m[c * P:(c + 1) * P, half * 512:(half + 1) * 512] for c in range(EC)]
        assert len(w_chunks) == W_B

        def w_target(n):
            if n < W_B:
                half, kind, c = n // (2 * EC), n // EC % 2, n % EC
                return (wa, wb)[kind][half], c
            kind, c = (n - W_B) // EC % 2, n % EC
            return (wa, wb)[kind][(n - W_B) // W_PER % 2], c

        def trans_bank(t):
            return trans_first[t] if t < BH else trans[t % 2]

        def heads(ap):
            return ap.rearrange("p (h k) -> p h k", h=HG)

        PASSES = ((0, 0), (0, 1), (1, 0))

        def project(pe, bank_, stationary, moving, ready=None):
            for c in range(EC):
                if ready is not None:
                    ready(c)
                for n, (s, m) in enumerate(PASSES):
                    mm = pe.matmul(bank_[:, :], stationary(s, c), moving(m, c),
                                   start=(c == 0 and n == 0), stop=(c == EC - 1 and n == 2))
            return mm

        def project_tile(pe, bank_, weights, h, source, half, ready=None):
            for c in range(EC):
                if ready is not None:
                    ready(c)
                for n, (s, m) in enumerate(PASSES):
                    mm = pe.matmul(bank_[:, :].rearrange("p (b t) -> p b t", b=BH),
                                   weights[s][:, c, h * P:(h + 1) * P],
                                   source[m][:, half * BH:(half + 1) * BH, c, :],
                                   start=(c == 0 and n == 0), stop=(c == EC - 1 and n == 2))
            return mm

        def q_lo_count(j, b, g):
            return j + (BH - (b - LAG_S) % BH)

        def groups(eng, unit):
            for b in range(B):
                unit(0, 0, b, b, False)
            with eng.Fori(1, KVH - 2, 2) as g:
                for par in (1, 0):
                    for b in range(B):
                        unit(g + (1 - par), par, b, B, False)
            for b in range(B):
                unit(KVH - 1, 1, b, B, False)
            for b in range(LAG_Y):
                unit(KVH, 0, b, B, True)

        def lagged(par, b, lag):
            return (par if b >= lag else 1 - par), (b - lag) % B

        def tile_a(m):
            if m < TILES_A - 2:
                keys, n = m % 2 == 0, m // 2
            else:
                keys, n = m < TILES_A, 2 * B - 2 + m % 2
            return keys, n // B, n % B, n

        def tile_after(keys, n):
            return [m for m in range(4 * B) if tile_a(m)[0] == keys and tile_a(m)[3] == n][0] + 1

        def slot_a(m):
            return (0, (TILES_A + NST - 1) // NST + 1) if m == 4 * B - 1 else (m % NST, m // NST)

        def q_split(s, g_half, h):
            flat = cT[s][:, :, :, :].rearrange("p b c t -> p (b c t)")
            at = (g_half % 2 * HG + h) * 512
            return flat[:, at:at + 512]

        def h_bank(hb):
            return qbank[hb % 2] if hb < BH else (sbank, tbank)[hb % 2]

        gate_bank = [pbank[0:8, :], obank[0:8, :]]
        gate_rows = [rot[0:8, hf, :] for hf in range(2)]

        def is_last(g, b):
            return isinstance(g, int) and g == KVH - 1

        def acts(a, s):
            return cT[a][:, (s % 2) * 4:(s % 2) * 4 + 4, :, :].rearrange("p b c t -> p b (c t)")

        def bcast(row, n):
            return row.rearrange("(a n) -> a n", a=1).to_broadcast([P, n])

        def store(sp, m):
            keys, half, k, _ = tile_a(m)
            slot, _ = slot_a(m)
            sp.wait_ge(u_lo, m + 1)
            for s in range(2):
                if keys:
                    dst = kv_scratch[half * HG + k % HG, k // HG * BH:(k // HG + 1) * BH, :, s, :]
                else:
                    dst = kv_scratch[half * HG:(half + 1) * HG, k, :, 2 + s, :]
                sp.dma_start(dst.rearrange("g p k -> p g k"),
                             heads(split[:, slot, s, :].bitcast(F32))).then_inc(stored[slot], 16)

        def expert_chunk(n):
            e, k = (n - W_C) // W_PER, (n - W_C) % W_PER
            return w1[e, k * P:(k + 1) * P, :] if k < EC else w2[e, (k - EC) * P:(k - EC + 1) * P, :]

        block = stack.enter_context(nc.Block())

        @block.sync
        def _(sp):
            def w_load(n, src):
                if n >= NW:
                    sp.wait_ge(w_lo, n - NW + 1)
                return sp.dma_start(wraw[:, n % NW, :], src)

            sp.dma_start(posi[:, :], pos.rearrange("b s -> s b"), allow_slow_non_contiguous=True
                         ).then_inc(pos_in, 16)
            for t in range(NROW):
                sp.dma_start(rows[:, t, :], ctx_in[t]).then_inc(row_in[t], 16)
            for n in range(W_DVE):
                w_load(n, w_chunks[n]).then_inc(w_in[n % NW], 16)
            for t in range(NROW, B):
                sp.wait_ge(row_t, t - NROW + 1)
                sp.dma_start(rows[:, t % NROW, :], ctx_in[t]).then_inc(row_in[t % NROW], 16)

            for m in range(-AHEAD, TILES_A):
                n = W_DVE + m + AHEAD
                if n < W_A:
                    src = w_chunks[n] if n < W_B else Wq[(n - W_B) * P:(n - W_B + 1) * P, 0:512]
                    w_load(n, src).then_inc(w_in[n % NW], 16)
                if m < 0:
                    continue
                if m < B:
                    sp.dma_start(xacc[:, m, :], x[m]).then_inc(x_in[m], 16)
                if m == B:
                    sp.dma_start(limit[:, :, :].bitcast(I32), mask.rearrange("b q k -> q b k")).then_inc(mask_in, 16)
                    sp.dma_start(gates[:, 0:1], bcast(g_xattn, 1)).then_inc(small_in, 16)
                    sp.dma_start(gates[:, 1:2], bcast(g_ffn, 1)).then_inc(small_in, 16)
                    sp.dma_start(gwm[:, 0, :], bcast(gate_w[E, :], NX)).then_inc(small_in, 16)
                    sp.dma_start(gwm[:, 1, :], bcast(gate_b, NX)).then_inc(small_in, 16)
                    sp.wait_ge(pool_const, 1)
                    sp.dma_start(gw[:, :, 0:NX], gate_w[0:E, :].rearrange("(c p) e -> p c e", p=P),
                                 allow_slow_non_contiguous=True).then_inc(small_in, 16)
                    for e in range(NX):
                        sp.dma_start(b1c[:, e, :], b1[e].rearrange("(c p) -> p c", p=P),
                                     allow_slow_non_contiguous=True).then_inc(small_in, 16)
                if m >= TILES_A - EC:
                    c = m - (TILES_A - EC)
                    w_load(W_A + c, Wo[c * P:(c + 1) * P, :]).then_inc(w_in[(W_A + c) % NW], 16)
                if m >= 1:
                    store(sp, m - 1)
            store(sp, TILES_A - 1)

            def unit(g, par, b, past, drain):
                i = g * B + b
                if not drain and past >= EC:
                    n = g * W_PER + (W_A + b)
                    sp.wait_ge(w_lo, n - NW + 1)
                    if b < EC:
                        src = Wo[bass.ds(g * 512 + b * P, P), :]
                    elif is_last(g, b):
                        src = w1[0, (b - EC) * P:(b - EC + 1) * P, :]
                    else:
                        src = Wq[(b - EC) * P:(b - EC + 1) * P, bass.ds(g * 512 + 512, 512)]
                    sp.dma_start(wraw[:, b % NW, :], src).then_inc(w_in[b % NW], 16)
                elif drain:
                    n = W_A + KVH * W_PER + b
                    w_load(n, expert_chunk(n)).then_inc(w_in[n % NW], 16)
                if past == LAG_S:
                    for k in range(NST):
                        sp.wait_ge(stored[k], 32 * (TILES_A // NST + (k == 0 and VALUES_AT[0] < LAG_S)))
                if past == LAG_S:
                    for u in range(KV_FIRST):
                        sp.dma_start(kv[:, u, :, :].bitcast(F32), kv_scratch[0, u]).then_inc(kv_in[u], 16)
                if past >= LAG_S + KV_FIRST and (not drain or b < LAG_S):
                    _, bj = lagged(par, b, LAG_S)
                    gj = g if b >= LAG_S else g - 1
                    if past - LAG_S >= NKV or past == B:
                        if not (isinstance(g, int) and i - LAG_S < NKV):
                            sp.wait_ge(o_done, i - LAG_S - NKV + 1 + (b == 0))
                    sp.dma_start(kv[:, bj % NKV, :, :].bitcast(F32), kv_scratch[gj, bj]
                                 ).then_inc(kv_in[bj % NKV], 16)
                if past in VALUES_AT:
                    store(sp, TILES_A + VALUES_AT.index(past))
                if past == B and b == 0:
                    sp.wait_ge(stored[0], 32 * (TILES_A // NST + 2))

            groups(sp, unit)

            sp.wait_ge(q_rot, UNITS)
            for e in range(NX):
                sp.dma_start(b2row[e], bcast(b2[e], E)).then_inc(b2_in, 16)
            for n in range(W_A + KVH * W_PER + LAG_Y, W_C + NX * W_PER):
                w_load(n, expert_chunk(n)).then_inc(w_in[n % NW], 16)
            for b in range(B):
                sp.wait_ge(f_acc, (NX - 1) * B + b + 1)
                sp.dma_start(out[b], xacc[:, b, :]).then_inc(out_done, 16)
            sp.wait_ge(out_done, 16 * B)

        @block.tensor
        def _(pe):
            def transpose4(bank_, src, done):
                for c in range(4):
                    mm = pe.transpose(bank_[:, c * P:(c + 1) * P], src(c), ident[:, :])
                mm.then_inc(done, 1)

            def row_transpose(t):
                if t < B:
                    pe.wait_ge(row_in[t % NROW], 16 * (t // NROW + 1))
                else:
                    pe.wait_ge(ln_row, t - B + 1)
                if t >= BH:
                    pe.wait_ge(row_lo, t - 1)
                transpose4(trans_bank(t), lambda c: rows[:, t % NROW, c * P:(c + 1) * P], row_t)

            def rope_transpose(k):
                pe.wait_ge(rope_in[k // 2], 16 * BH)
                if k >= 2:
                    pe.wait_ge(rope_ok, k - 1)
                src = rope_rows_sb[k // 2]
                transpose4(rope_bank[k % 2], lambda c: src[:, 2 * (k % 2) + c // 2, c % 2 * P:(c % 2 + 1) * P], rope_t)

            pe.wait_ge(ident_ok, 2)
            for t in range(BH):
                row_transpose(t)
            def chunk_ready(first):
                return lambda c: pe.wait_ge(w_lo, first + c + 1)

            def value_tile(n, ready=None):
                if n >= 2:
                    pe.wait_ge(u_lo, tile_after(False, n - 2))
                if n == 1:
                    pe.wait_ge(rope_ok, 4)
                project(pe, ybank[n % 2], lambda s, c: cT[s][:, n % B, c, :],
                        lambda s, c: wb[n // B][s][:, c, :], ready=ready).then_inc(v_proj, 1)

            for m in range(TILES_A):
                keys, half, k, n = tile_a(m)
                if m == 0:
                    pe.wait_ge(row_lo, BH)
                elif keys and k == HG and half == 0:
                    pe.wait_ge(row_lo, B)
                ready = None
                if n == 0:
                    ready = chunk_ready(m * EC)
                elif k == 0:
                    pe.wait_ge(w_lo, (2 * half + (not keys) + 1) * EC)
                if keys:
                    if n >= 2:
                        pe.wait_ge(k_rot, n - 1)
                    project_tile(pe, qbank[n % 2], wa[half], k % HG, cT, k // HG, ready=ready).then_inc(k_proj, 1)
                    if m == 0:
                        rope_transpose(0)
                        rope_transpose(1)
                    if m < B:
                        row_transpose(BH + m // 2)
                    if m >= 2 * B:
                        row_transpose(n)
                else:
                    value_tile(n, ready)
                    if n == 0:
                        rope_transpose(2)
                        rope_transpose(3)

            def unit(g, par, b, past, drain):
                i = g * B + b

                def has(lag):
                    return past >= lag and (not drain or b < lag)

                if has(LAG_S):
                    _, bs = lagged(par, b, LAG_S)
                    pe.wait_ge(q_lo, q_lo_count(i - LAG_S, b, g))
                    pe.wait_ge(kv_in[bs % NKV], (g * 2 + ((b - LAG_S) // NKV + 1)) * 16)
                    if past >= LAG_S + 1:
                        pe.wait_ge(s_sum, i - LAG_S)
                    for h in range(HG):
                        q = [q_split(s, bs // BH, h)[:, bs % BH * P:(bs % BH + 1) * P] for s in range(2)]
                        pe.matmul(sbanks[:, 2 * h * P:(2 * h + 2) * P], q[0],
                                  kv[:, bs % NKV, 0:2, :].rearrange("p m k -> p (m k)"), start=True, stop=False)
                        mm = pe.matmul(sbanks[:, 2 * h * P:(2 * h + 1) * P], q[1], kv[:, bs % NKV, 0, :],
                                       start=False, stop=True)
                    mm.then_inc(s_done, 1)
                if has(0):
                    if b == 0:
                        pe.wait_ge(w_lo, g * W_PER + (W_B + EC))
                    if past == 0:
                        pe.wait_ge(row_lo, B + BH)
                    if past == BH:
                        pe.wait_ge(row_lo, 2 * B)
                    if past >= 2:
                        pe.wait_ge(q_rot, i - 1)
                    else:
                        pe.wait_ge(k_rot, 2 * B - 1 + past)
                if has(0):
                    project_tile(pe, qbank[b % 2], wa[par], b % HG, xT, b // BH).then_inc(q_proj, 1)
                if has(LAG_P):
                    pe.wait_ge(p_norm, i - LAG_P + 1)
                    if past >= LAG_P + 1:
                        pe.wait_ge(p_lo, i - LAG_P)
                    transpose4(pbank, lambda c: prob[:, 1, c * P:(c + 1) * P], p_t)
                if past in VALUES_IN:
                    value_tile(2 * B - 2 + VALUES_IN.index(past))
                if drain and b == LAG_Y - 1:
                    gate_products(0)
                    first_layer(0, 1)
                if not drain and past == LAG_Y:
                    pe.wait_ge(u_lo, TILES_A + 1)
                if has(LAG_Y):
                    p3, b3 = lagged(par, b, LAG_Y)
                    pe.wait_ge(o_lo, i - LAG_Y + 1)
                    if b3 == 0:
                        pe.wait_ge(w_lo, g * W_PER + (W_B + W_PER))
                    if not (isinstance(g, int) and i - LAG_Y < 2):
                        pe.wait_ge(y_acc, i - LAG_Y - 1 + (b == 0))
                    project(pe, ybank[b3 % 2], lambda s, c: split[:, 2, s, c * P:(c + 1) * P],
                            lambda s, c: wb[p3][s][:, c, :]).then_inc(y_done, 1)
                if drain and b == LAG_Y - 2:
                    first_layer(0, 0)
                if drain and b >= 1:
                    h_transpose(b - 1)
                if not drain and past == LAG_Y:
                    pe.wait_ge(u_lo, 4 * B)
                if has(LAG_P):
                    _, bs = lagged(par, b, LAG_P)
                    pe.wait_ge(p_lo, i - LAG_P + 1)
                    if past >= LAG_P + 1:
                        pe.wait_ge(o_lo, i - LAG_P)
                    for n, (s, m) in enumerate(PASSES):
                        mm = pe.matmul(obank[:, :], kv[:, bs % NKV, 2 + s, :], split[:, 1, m, :],
                                       start=(n == 0), stop=(n == 2))
                    mm.then_inc(o_done, 1)

            def h_transpose(hb):
                pe.wait_ge(h_row, hb + 1)
                if hb == 0:
                    pe.wait_ge(q_rot, UNITS)
                elif hb == BH:
                    pe.wait_ge(s_sum, UNITS)
                if hb % BH >= 2:
                    pe.wait_ge(h_lo, hb - 1)
                transpose4(h_bank(hb), lambda c: rows[:, hb % NROW, c * P:(c + 1) * P], h_t)

            def gate_products(hf):
                if hf == 0:
                    pe.wait_ge(gw_lo, 1)
                    pe.wait_ge(p_lo, UNITS)
                else:
                    pe.wait_ge(o_lo, UNITS)
                pe.wait_ge(h_lo, (hf + 1) * BH)
                for c in range(EC):
                    for m in range(2):
                        mm = pe.matmul(gate_bank[hf][:, :].rearrange("p (b t) -> p b t", b=BH), gws[:, c, :],
                                       xT[m][:, hf * BH:(hf + 1) * BH, c, :],
                                       start=(c == 0 and m == 0), stop=(c == EC - 1 and m == 1))
                mm.then_inc(gate_mm, 1)

            def first_layer(s, f):
                e, hf, l = s // 2, s % 2, s * EC + f
                if hf == 0 and f == 0:
                    pe.wait_ge(w_lo, W_C + e * W_PER + EC)
                if l == 0:
                    pe.wait_ge(h_lo, BH)
                if l == EC:
                    pe.wait_ge(h_lo, B)
                if l < 2:
                    pe.wait_ge(q_rot, UNITS)
                else:
                    pe.wait_ge(f_act, l - 1)
                project_tile(pe, qbank[l % 2], wa[e % 2], f, xT, hf).then_inc(f1, 1)

            groups(pe, unit)

            def second_layer(s):
                e, hf = s // 2, s % 2
                if hf == 0:
                    pe.wait_ge(w_lo, W_C + (e + 1) * W_PER)
                pe.wait_ge(f_lo, (s + 1) * EC)
                for k in range(4):
                    u = s * 4 + k
                    if u < 2:
                        pe.wait_ge(y_acc, UNITS - 1 + u)
                    else:
                        pe.wait_ge(f_acc, u - 1)
                    project(pe, ybank[u % 2],
                            lambda a, c: acts(a, s)[:, c, k * P:(k + 1) * P],
                            lambda a, c: wb[e % 2][a][:, c, :]).then_inc(f2, 1)

            def router():
                pe.wait_ge(fold_ok, 1)
                pe.wait_ge(gate_in, 2)
                pe.wait_ge(s_sum, UNITS)
                for b in range(B):
                    pe.matmul(sbank[:, 4 * b:4 * b + 4], gate_rows[b // BH][:, b % BH * P:(b % BH + 1) * P],
                              fold[:, :], start=True, stop=True)
                pe.wait_ge(h_abs, B)
                for k in range(2):
                    mm = pe.matmul(sbank[:, 64 + B * k:64 + B * (k + 1)], sel[:, k, :], absum[:, :],
                                   start=True, stop=True)
                mm.then_inc(route_mm, 1)

            def token0():
                pe.wait_ge(tok0_in, 1)
                pe.matmul(sbank[:, 128:128 + B * NX], sel[:, 2, :], score.rearrange("p b e -> p (b e)"),
                          start=True, stop=True).then_inc(tok0_mm, 1)

            h_transpose(B - 2)
            first_layer(0, 2)
            h_transpose(B - 1)
            first_layer(0, 3)
            gate_products(1)
            for f in range(EC):
                first_layer(1, f)
                if f == 0:
                    router()
                if f == 2:
                    token0()
            for s in range(2, 2 * NX):
                second_layer(s - 2)
                for f in range(EC):
                    first_layer(s, f)
            second_layer(2 * NX - 2)
            second_layer(2 * NX - 1)

        @block.scalar
        def _(act):
            def w_split_hi(n, k, dst):
                act.wait_ge(w_in[k], (n // NW + 1) * 16)
                act.activation(dst, wraw[:, k, :], ACT.Copy).then_inc(w_hi, 1)

            def norm_row(which, b):
                if which == 0:
                    act.wait_ge(ln_nmr, 1)
                    act.wait_ge(row_t, max(B, B + b - NROW + 1))
                else:
                    act.wait_ge(h_nmr, b + 1)
                    if b >= NROW:
                        act.wait_ge(h_t, b - NROW + 1)
                    else:
                        act.wait_ge(row_t, 2 * B)
                act.activation(rows[:, b % NROW, :], xacc[:, b, :], ACT.Identity, bias=nmr[:, which, b:b + 1],
                               scale=rstd[:, which, b:b + 1]).then_inc((ln_row, h_row)[which], 1)

            def row_hi_(t):
                act.wait_ge(row_t, t + 1)
                dst = (cT if t < B else xT)[0][:, t % B, :, :]
                act.activation(dst.rearrange("p c t -> p (c t)"), trans_bank(t)[:, :], ACT.Copy).then_inc(row_hi, 1)

            def tile_hi(m):
                keys, half, k, n = tile_a(m)
                slot, before = slot_a(m)
                if before:
                    act.wait_ge(stored[slot], 32 * before)
                if keys:
                    act.wait_ge(k_roped, n + 1)
                    act.activation(split[:, slot, 0, :], roped[:, :], ACT.Copy, scale=SCALE).then_inc(u_hi, 1)
                else:
                    act.wait_ge(v_proj, n + 1)
                    act.activation(split[:, slot, 0, :], ybank[n % 2][:, :], ACT.Copy).then_inc(u_hi, 1)

            def rope_copy(k):
                act.wait_ge(rope_t, k + 1)
                act.activation(rope[:, :, 2 * k:2 * k + 2, :],
                               rope_bank[k % 2][:, :].rearrange("p (b c t) -> p c b t", b=2, c=2), ACT.Copy
                               ).then_inc(rope_ok, 1)

            def w_hi_to(n):
                buf, c = w_target(n)
                w_split_hi(n, n % NW, buf[0][:, c, :])

            for t in range(BH):
                row_hi_(t)
            for n in range(W_DVE):
                w_hi_to(n)
            rope_copy(0)
            rope_copy(1)
            for m in range(TILES_A):
                keys, _, _, n = tile_a(m)
                if m < B and keys:
                    row_hi_(BH + n)
                if m >= 2 * B and keys:
                    row_hi_(n)
                    if n < 2 * B - 2:
                        norm_row(0, n - B + 2)
                if m < 2 * EC:
                    w_hi_to(W_DVE + m)
                if 2 * B <= m < 2 * B + EC:
                    if m == 2 * B:
                        act.wait_ge(k_proj, B)
                    w_hi_to(W_B + m - 2 * B)
                if m == 3 * B:
                    act.wait_ge(small_in, 16 * 8)
                    act.activation(gates[:, :], gates[:, :], ACT.Tanh).then_inc(gates_ok, 1)
                    act.activation(gws[:, :, 0:4], gw[:, :, :], ACT.Copy).then_inc(gw_hi, 1)
                if m == 1:
                    rope_copy(2)
                    rope_copy(3)
                if m == 2 * B - 1:
                    norm_row(0, 0)
                    norm_row(0, 1)
                if not keys:
                    tile_hi(m - 1)
                    tile_hi(m)
                if m >= TILES_A - 2:
                    tile_hi(m)
            def unit(g, par, b, past, drain):
                i = g * B + b

                def has(lag):
                    return past >= lag and (not drain or b < lag)

                if past == LAG_P:
                    for k in (1, 2):
                        act.wait_ge(stored[k], 32 * (TILES_A // NST))
                if past in VALUES_AT:
                    tile_hi(TILES_A + VALUES_AT.index(past))
                if has(LAG_Y):
                    act.wait_ge(o_done, i - LAG_Y + 1)
                    if not (isinstance(g, int) and i - LAG_Y < 1):
                        act.wait_ge(y_done, i - LAG_Y)
                    act.activation(split[:, 2, 0, :], obank[:, :], ACT.Copy).then_inc(o_hi, 1)
                if has(LAG_S):
                    act.wait_ge(s_done, i - LAG_S + 1)
                    if past >= LAG_S + 1:
                        act.wait_ge(s_exp, i - LAG_S)
                    act.activation(heads(scores[:, :]), score_parts[:, :, 1, :], ACT.Copy).then_inc(s_part, 1)
                if not drain:
                    if b == 0 and past >= B:
                        act.wait_ge(y_done, g * B - B + 1)
                    if b == EC:
                        if past >= B:
                            act.wait_ge(q_proj, g * B)
                        else:
                            act.wait_ge(k_proj, 2 * B)
                    buf = wb[par] if b < EC else wa[1 - par]
                    act.wait_ge(w_in[b % NW], (g * 2 + ((W_A + b) // NW + 1)) * 16)
                    act.activation(buf[0][:, b % EC, :], wraw[:, b % NW, :], ACT.Copy).then_inc(w_hi, 1)
                else:
                    if b >= 2:
                        h_hi_(b - 2)
                    if b == EC:
                        act.wait_ge(q_proj, UNITS)
                    w_expert_hi(W_A + KVH * W_PER + b)
                if drain and b >= 1:
                    norm_row(1, b - 1)
                if has(1):
                    _, bq = lagged(par, b, 1)
                    act.wait_ge(q_roped, i)
                    if past >= B:
                        act.wait_ge(s_done, s_done_before(i - 1, bq))
                    act.activation(q_split(0, bq // BH, bq % HG), roped[:, :], ACT.Copy).then_inc(q_hi, 1)
                if has(LAG_P):
                    act.wait_ge(p_t, i - LAG_P + 1)
                    if past >= LAG_P + 1:
                        act.wait_ge(o_done, i - LAG_P)
                    act.activation(split[:, 1, 0, :], pbank[:, :], ACT.Copy).then_inc(p_hi, 1)
                if has(LAG_S):
                    act.wait_ge(s_max, i - LAG_S + 1)
                    if past >= LAG_S + 1:
                        act.wait_ge(p_norm, i - LAG_S)
                    turn = (b - LAG_S) % 2
                    for h in range(HG):
                        a = act.activation(prob[:, 0, h * P:(h + 1) * P], scores[:, h * P:(h + 1) * P], ACT.Exp,
                                           bias=nmax[:, turn, h:h + 1], accum_out=psums[:, turn, h:h + 1])
                    a.then_inc(s_exp, 1)
                if drain:
                    if b >= 2:
                        sum_abs(b - 2)
                    if b == LAG_Y - 1:
                        norm_row(1, b)
                        h_hi_(b - 1)
                    if b >= LAG_S:
                        activation_chunk(0, b - LAG_S)

            def s_done_before(t, bq):
                return t - bq % BH - BH + (bq == B - 1)

            def w_expert_hi(n):
                e, k = (n - W_C) // W_PER, (n - W_C) % W_PER
                w_split_hi(n, n % NW, (wa if k < EC else wb)[e % 2][0][:, k % EC, :])

            def gate_copy(hf):
                act.wait_ge(gate_mm, hf + 1)
                act.activation(gate_rows[hf], gate_bank[hf], ACT.Copy).then_inc(gate_in, 1)

            def sum_abs(hb):
                if hb >= 1:
                    act.wait_ge(h_abs, hb)
                act.wait_ge(h_row, hb + 1)
                act.activation(unread, rows[:, hb % NROW, :], ACT.Abs, accum_out=absum[:, hb:hb + 1]
                               ).then_inc(h_abs, 1)

            def h_hi_(hb):
                act.wait_ge(h_t, hb + 1)
                act.activation(xT[0][:, hb, :, :].rearrange("p c t -> p (c t)"), h_bank(hb)[:, :], ACT.Copy
                               ).then_inc(h_hi, 1)

            def activation_chunk(s, f):
                l, e = s * EC + f, s // 2
                act.wait_ge(f1, l + 1)
                if l < 2:
                    act.wait_ge(p_t, UNITS)
                else:
                    act.wait_ge(f_lo, l - 1)
                func = (ACT.Tanh, ACT.Gelu, ACT.Silu)[e]
                act.activation(prob[:, l % 2, :], qbank[l % 2][:, :], func, bias=b1c[:, e, f:f + 1]
                               ).then_inc(f_act, 1)
                act.wait_ge(f_act, l + 1)
                if s >= 2 and f == 0:
                    act.wait_ge(f2, (s - 1) * 4)
                act.activation(acts(0, s)[:, f, :], prob[:, l % 2, :], ACT.Copy).then_inc(f_hi, 1)

            groups(act, unit)

            n = W_A + KVH * W_PER + LAG_Y
            h_hi_(B - 2)
            norm_row(1, B - 1)
            w_expert_hi(n)
            gate_copy(0)
            activation_chunk(0, 2)
            h_hi_(B - 1)
            for b in range(B - 3, B):
                sum_abs(b)
            activation_chunk(0, 3)
            for l in range(EC, 2 * NX * EC):
                s, f = l // EC, l % EC
                if s == 1 and f == 0:
                    gate_copy(1)
                if s >= 1:
                    activation_chunk(s, f)
                if s == 1 and f == 0:
                    act.wait_ge(score_exp_in, 1)
                    act.activation(exps, logit, ACT.Exp).then_inc(score_exp, 1)
                n += 1
                if n < W_C + NX * W_PER:
                    if n == W_C + W_PER + EC:
                        act.wait_ge(y_done, UNITS)
                    if n == W_C + 2 * W_PER:
                        act.wait_ge(f1, 2 * EC)
                    if n == W_C + 2 * W_PER + EC:
                        act.wait_ge(f2, B)
                    w_expert_hi(n)

        @block.gpsimd
        def _(pool):
            pool.memset(gw[:, :, :], 0.0).then_inc(pool_const, 1)
            pool.memset(ident[:, :], 0.0).then_inc(ident_ok, 1)
            pool.wait_ge(ident_ok, 1)
            pool.affine_select(out=ident[:, :], in_=ident[:, :], compare_op=ALU.not_equal, fill=1.0, base=0,
                               pattern=[[-1, P]], channel_multiplier=1).then_inc(ident_ok, 1)
            pool.memset(mhalf[:, :], -0.5).then_inc(pool_const, 1)
            pool.memset(sel[:, :, :], 1.0).then_inc(pool_const, 1)
            pool.wait_ge(pool_const, 3)
            pool.affine_select(out=sel[:, 0, :], in_=sel[:, 0, :], compare_op=ALU.is_ge, fill=0.0, base=-VISION,
                               pattern=[[0, P]], channel_multiplier=1).then_inc(pool_const, 1)
            pool.affine_select(out=sel[:, 1, :], in_=sel[:, 1, :], compare_op=ALU.is_gt, fill=0.0, base=VISION,
                               pattern=[[0, P]], channel_multiplier=-1).then_inc(pool_const, 1)
            pool.affine_select(out=sel[:, 2, :], in_=sel[:, 2, :], compare_op=ALU.is_gt, fill=0.0, base=1,
                               pattern=[[0, P]], channel_multiplier=-1).then_inc(pool_const, 1)

            pool.wait_ge(pos_ok, 1)
            for b in range(B):
                pool.indirect_dma_start(rope_rows_sb[b // BH][:, b % BH, :], None, rope_rows[:, :],
                                        bass.IndirectOffsetOnAxis(ap=posi[:, b:b + 1], axis=0)
                                        ).then_inc(rope_in[b // BH], 16)

            def w_split_lo(n, buf, c):
                pool.wait_ge(w_hi, n + 1)
                pool.tensor_tensor(buf[1][:, c, :], wraw[:, n % NW, :], buf[0][:, c, :].bitcast(F32), ALU.subtract
                                   ).then_inc(w_lo, 1)

            def w_expert_lo(n):
                e, k = (n - W_C) // W_PER, (n - W_C) % W_PER
                w_split_lo(n, (wa if k < EC else wb)[e % 2], k % EC)

            pool.wait_ge(w_lo, W_DVE)
            for m in range(TILES_A):
                keys, half, k, n = tile_a(m)
                if keys:
                    pool.wait_ge(k_rot, n + 1)
                    if n >= 1:
                        pool.wait_ge(u_lo, tile_after(True, n - 1))
                    pool.tensor_tensor(roped[:, :], rot[:, 0, :], rot[:, 1, :], ALU.add).then_inc(k_roped, 1)
                if m < 2 * EC:
                    w_split_lo(W_DVE + m, *w_target(W_DVE + m))
                if 2 * B <= m < 2 * B + EC:
                    w_split_lo(W_B + m - 2 * B, *w_target(W_B + m - 2 * B))
                if m == 2 * B - 3:
                    pool.wait_ge(ln_var, 1)
                    pool.tensor_tensor(rstd[:, 0, :], rstd[:, 0, :], mhalf[:, :], ALU.pow).then_inc(ln_rstd, 1)

            def unit(g, par, b, past, drain):
                i = g * B + b

                def has(lag):
                    return past >= lag and (not drain or b < lag)

                def weight_lo():
                    buf = wb[par] if b < EC else wa[1 - par]
                    pool.wait_ge(w_hi, g * W_PER + (W_A + b + 1))
                    pool.tensor_tensor(buf[1][:, b % EC, :], wraw[:, b % NW, :],
                                       buf[0][:, b % EC, :].bitcast(F32), ALU.subtract).then_inc(w_lo, 1)

                if has(1):
                    _, bq = lagged(par, b, 1)
                    if past > FILL:
                        pool.wait_ge(q_rot, i)
                        pool.wait_ge(q_lo, i - 1)
                        pool.tensor_tensor(roped[:, :], rot[:, 0, :], rot[:, 1, :], ALU.add).then_inc(q_roped, 1)
                        if not drain:
                            weight_lo()
                    pool.wait_ge(q_hi, i)
                    pool.tensor_tensor(q_split(1, bq // BH, bq % HG), roped[:, :],
                                       q_split(0, bq // BH, bq % HG).bitcast(F32), ALU.subtract).then_inc(q_lo, 1)
                if past <= FILL:
                    weight_lo()
                if has(LAG_S):
                    turn = (b - LAG_S) % 2
                    pool.wait_ge(s_rec, i - LAG_S + 1)
                    if past >= LAG_S + 1:
                        pool.wait_ge(p_t, i - LAG_S)
                    pool.tensor_tensor(heads(prob[:, 1, :]), heads(prob[:, 0, :]),
                                       prec[:, turn, :].unsqueeze(2).to_broadcast([P, HG, P]), ALU.mult
                                       ).then_inc(p_norm, 1)
                if drain:
                    h_pow(b)
                    w_expert_lo(W_A + KVH * W_PER + b)
                    if b == LAG_Y - 1:
                        h_pow(B - 1)
                    if b >= LAG_S:
                        activation_lo(b - LAG_S)

            def h_pow(hb):
                pool.wait_ge(h_var, hb + 1)
                pool.tensor_tensor(rstd[:, 1, hb:hb + 1], rstd[:, 1, hb:hb + 1], mhalf[:, 0:1], ALU.pow
                                   ).then_inc(h_rstd, 1)

            def activation_lo(l):
                s, f = l // EC, l % EC
                pool.wait_ge(f_hi, l + 1)
                pool.tensor_tensor(acts(1, s)[:, f, :], prob[:, l % 2, :], acts(0, s)[:, f, :].bitcast(F32),
                                   ALU.subtract).then_inc(f_lo, 1)

            groups(pool, unit)

            n = W_A + KVH * W_PER + LAG_Y
            w_expert_lo(n)
            activation_lo(2)
            activation_lo(3)
            for l in range(EC, 2 * NX * EC):
                activation_lo(l)
                n += 1
                if n < W_C + NX * W_PER:
                    w_expert_lo(n)

        @block.vector
        def _(dve):
            def subtract_hi(dst, src, hi, done):
                dve.tensor_tensor(dst, src, hi.bitcast(F32), ALU.subtract).then_inc(done, 1)

            def row_lo_(t):
                dve.wait_ge(row_hi, t + 1)
                T = cT if t < B else xT
                subtract_hi(T[1][:, t % B, :, :].rearrange("p c t -> p (c t)"), trans_bank(t)[:, :],
                            T[0][:, t % B, :, :].rearrange("p c t -> p (c t)"), row_lo)

            def tile_lo(m):
                keys, half, k, n = tile_a(m)
                dve.wait_ge(u_hi, m + 1)
                slot, _ = slot_a(m)
                hi, lo = split[:, slot, 0, :], split[:, slot, 1, :]
                if keys:
                    dve.scalar_tensor_tensor(out=lo, in0=roped[:, :], scalar=SCALE, in1=hi.bitcast(F32),
                                             op0=ALU.mult, op1=ALU.subtract).then_inc(u_lo, 1)
                else:
                    subtract_hi(lo, ybank[n % 2][:, :], hi, u_lo)

            def rotate(bank_, half, done):
                def table(k, a, z):
                    return rope[a:z, k, half * BH:(half + 1) * BH, :].rearrange("p b t -> p (b t)")

                dve.tensor_tensor(rot[:, 0, :], bank_[:, :], table(0, 0, D), ALU.mult)
                dve.tensor_tensor(rot[0:HALF, 1, :], bank_[HALF:D, :], table(1, HALF, D), ALU.mult)
                dve.tensor_tensor(rot[HALF:D, 1, :], bank_[0:HALF, :], table(1, 0, HALF), ALU.mult
                                  ).then_inc(done, 1)

            dve.wait_ge(pos_in, 16)
            dve.tensor_copy(posf[:, 0, :], posi[:, :]).then_inc(pos_step, 1)
            dve.wait_ge(pos_step, 1)
            dve.tensor_scalar(posf[:, 1, :], posf[:, 0, :], 0.0, float(MAX_POS), ALU.is_lt, ALU.mult
                              ).then_inc(pos_step, 1)
            dve.wait_ge(pos_step, 2)
            dve.tensor_tensor(posf[:, 2, :], posf[:, 0, :], posf[:, 1, :], ALU.add).then_inc(pos_step, 1)
            dve.wait_ge(pos_step, 3)
            dve.tensor_scalar(posi[:, :], posf[:, 2, :], 0.0, float(MAX_POS - 1), ALU.max, ALU.min
                              ).then_inc(pos_ok, 1)

            for t in range(BH):
                row_lo_(t)
            for n in range(W_DVE):
                buf, c = w_target(n)
                dve.wait_ge(w_hi, n + 1)
                subtract_hi(buf[1][:, c, :], wraw[:, n % NW, :], buf[0][:, c, :], w_lo)
            for m in range(TILES_A):
                keys, half, k, n = tile_a(m)
                if keys:
                    if n == 0:
                        dve.wait_ge(rope_ok, 2)
                        dve.wait_ge(rope_t, 2)
                    else:
                        dve.wait_ge(k_roped, n)
                    if n == HG:
                        dve.wait_ge(rope_ok, 4)
                    dve.wait_ge(k_proj, n + 1)
                    rotate(qbank[n % 2], k // HG, k_rot)
                    if m < B:
                        row_lo_(BH + n)
                    for k in range(max(0, m - (2 if m < TILES_A - 1 else 1)), m):
                        tile_lo(k)
                    if m >= 2 * B:
                        row_lo_(n)
                else:
                    if LN_FROM <= m < LN_FROM + B:
                        for t in (m - LN_FROM, m - LN_FROM + 1):
                            dve.wait_ge(x_in[t], 16)
                            dve.bn_stats(bn[:, 0, t, :], xacc[:, t, :]).then_inc(ln_step, 1)
                            dve.wait_ge(ln_step, 2 * t + 1)
                            dve.bn_aggr(mv[:, 0, t, :], bn[:, 0, t, :]).then_inc(ln_step, 1)
                    if m == LN_FROM + B - 2:
                        dve.wait_ge(ln_step, 2 * B)
                        dve.tensor_scalar(rstd[:, 0, :], mv[:, 0, :, 1], LN_EPS, None, ALU.add).then_inc(ln_var, 1)
                    if m == LN_FROM + B:
                        dve.wait_ge(ln_rstd, 1)
                        dve.scalar_tensor_tensor(out=nmr[:, 0, :], in0=mv[:, 0, :, 0], scalar=-1.0,
                                                 in1=rstd[:, 0, :], op0=ALU.mult, op1=ALU.mult).then_inc(ln_nmr, 1)
                if m == 3 * B + 1:
                    dve.wait_ge(gw_hi, 1)
                    subtract_hi(gws[:, :, 4:8], gw[:, :, :], gws[:, :, 0:4], gw_lo)
                    dve.wait_ge(ident_ok, 2)
                    dve.tensor_tensor(fold[:, :], ident[0:8, 0:4], ident[0:8, 4:8], ALU.add).then_inc(fold_ok, 1)
                if m == 2 * B + 1:
                    keep = prob[:, :, :].rearrange("p t (b k) -> p (t b) k", b=HG)
                    raw = limit[:, :, :].bitcast(I32)
                    dve.wait_ge(mask_in, 16)
                    dve.tensor_scalar(keep, raw, 0.0, KEEP, ALU.not_equal, ALU.mult).then_inc(lim_step, 1)
                    dve.wait_ge(lim_step, 1)
                    dve.tensor_scalar(limit[:, :, :], raw, 0.0, MASKED, ALU.is_equal, ALU.mult).then_inc(lim_step, 1)
                    dve.wait_ge(lim_step, 2)
                    dve.tensor_tensor(limit[:, :, :], limit[:, :, :], keep, ALU.add).then_inc(limit_ok, 1)
            dve.wait_ge(gates_ok, 1)
            dve.wait_ge(limit_ok, 1)
            dve.wait_ge(k_roped, 2 * B)

            def unit(g, par, b, past, drain):
                i = g * B + b

                def has(lag):
                    return past >= lag and (not drain or b < lag)

                if has(1):
                    _, bq = lagged(par, b, 1)
                    dve.wait_ge(q_proj, i)
                    if past >= 2:
                        dve.wait_ge(q_roped, i - 1)
                    rotate(qbank[bq % 2], bq // BH, q_rot)
                    if past == 1:
                        tile_lo(TILES_A - 1)
                        dve.wait_ge(u_lo, TILES_A)
                    if past <= FILL:
                        dve.wait_ge(q_rot, i)
                        if past >= 2:
                            dve.wait_ge(q_lo, i - 1)
                        dve.tensor_tensor(roped[:, :], rot[:, 0, :], rot[:, 1, :], ALU.add).then_inc(q_roped, 1)
                if has(LAG_Y):
                    dve.wait_ge(o_hi, i - LAG_Y + 1)
                    subtract_hi(split[:, 2, 1, :], obank[:, :], split[:, 2, 0, :], o_lo)
                if drain and b >= 1:
                    h_neg_mean(b - 1)
                if past in VALUES_AT:
                    tile_lo(TILES_A + VALUES_AT.index(past))
                if has(LAG_S):
                    turn, bs = (b - LAG_S) % 2, (b - LAG_S) % B
                    dve.wait_ge(s_part, i - LAG_S + 1)
                    dve.tensor_tensor(heads(scores[:, :]), score_parts[:, :, 0, :], heads(scores[:, :]),
                                      ALU.add).then_inc(s_sum, 1)
                    dve.wait_ge(s_sum, i - LAG_S + 1)
                    dve.tensor_tensor(heads(scores[:, :]), heads(scores[:, :]),
                                      limit[:, bs, :].unsqueeze(1).to_broadcast([P, HG, P]), ALU.min
                                      ).then_inc(s_limited, 1)
                    dve.wait_ge(s_limited, i - LAG_S + 1)
                    dve.tensor_reduce(nmax[:, turn, :], heads(scores[:, :]), AX.X, ALU.max, negate=True
                                      ).then_inc(s_max, 1)
                if has(LAG_P):
                    dve.wait_ge(p_hi, i - LAG_P + 1)
                    subtract_hi(split[:, 1, 1, :], pbank[:, :], split[:, 1, 0, :], p_lo)
                if drain:
                    if b >= 2:
                        h_lo_(b - 2)
                    h_stats(b)
                    if b == LAG_Y - 1:
                        h_neg_mean(b)
                if has(LAG_S):
                    turn = (b - LAG_S) % 2
                    dve.wait_ge(s_exp, i - LAG_S + 1)
                    dve.reciprocal(prec[:, turn, :], psums[:, turn, :]).then_inc(s_rec, 1)
                if has(LAG_Y):
                    b3 = (b - LAG_Y) % B
                    dve.wait_ge(y_done, i - LAG_Y + 1)
                    dve.scalar_tensor_tensor(out=xacc[:, b3, :], in0=ybank[b3 % 2][:, :], scalar=gates[:, 0:1],
                                             in1=xacc[:, b3, :], op0=ALU.mult, op1=ALU.add).then_inc(y_acc, 1)
            def h_lo_(hb):
                dve.wait_ge(h_hi, hb + 1)
                subtract_hi(xT[1][:, hb, :, :].rearrange("p c t -> p (c t)"), h_bank(hb)[:, :],
                            xT[0][:, hb, :, :].rearrange("p c t -> p (c t)"), h_lo)

            def h_stats(hb):
                dve.wait_ge(y_acc, UNITS - B + hb + 1)
                dve.bn_stats(bn[:, 1, hb, :], xacc[:, hb, :]).then_inc(h_step, 1)
                dve.wait_ge(h_step, 2 * hb + 1)
                dve.bn_aggr(mv[:, 1, hb, :], bn[:, 1, hb, :]).then_inc(h_step, 1)
                dve.wait_ge(h_step, 2 * hb + 2)
                dve.tensor_scalar(rstd[:, 1, hb:hb + 1], mv[:, 1, hb, 1:2], LN_EPS, None, ALU.add
                                  ).then_inc(h_var, 1)

            def h_neg_mean(hb):
                dve.wait_ge(h_rstd, hb + 1)
                dve.scalar_tensor_tensor(out=nmr[:, 1, hb:hb + 1], in0=mv[:, 1, hb, 0:1], scalar=-1.0,
                                         in1=rstd[:, 1, hb:hb + 1], op0=ALU.mult, op1=ALU.mult).then_inc(h_nmr, 1)

            groups(dve, unit)
            h_stats(B - 1)
            h_lo_(B - 3)
            h_neg_mean(B - 1)
            h_lo_(B - 2)
            h_lo_(B - 1)

            steps = [0]

            def then(ins):
                ins.then_inc(route_step, 1)
                steps[0] += 1
                dve.wait_ge(route_step, steps[0])

            def tt(o, a, b_, op):
                then(dve.tensor_tensor(o, a, b_, op))

            def ts(o, a, s1, s2, op0, op1=ALU.bypass):
                then(dve.tensor_scalar(o, a, s1, s2, op0, op1) if s2 is not None
                     else dve.tensor_scalar(o, a, s1, None, op0))

            def over_e(ap):
                return ap.unsqueeze(2).to_broadcast([P, B, NX])

            def over_b(ap):
                return ap.unsqueeze(1).to_broadcast([P, B, NX])

            dve.wait_ge(route_mm, 1)
            ts(text, sbank[:, 64:64 + B], 1.0 / ((P - VISION) * E), None, ALU.mult)
            ts(vision, sbank[:, 64 + B:64 + 2 * B], 1.0 / (VISION * E), 1e-8, ALU.mult, ALU.add)
            then(dve.reciprocal(ratio, vision))
            tt(ratio, ratio, text, ALU.mult)
            tt(part, over_e(ratio), over_b(gwm[:, 0, :]), ALU.mult)
            tt(logit_sum, part,
               sbank[:, 0:4 * B].rearrange("p (b e) -> p b e", e=4)[:, :, 0:NX], ALU.add)
            tt(part, logit_sum, over_b(gwm[:, 1, :]), ALU.add)
            then(dve.tensor_reduce(logit_max, part, AX.X, ALU.max))
            dve.tensor_tensor(logit, part, over_e(logit_max), ALU.subtract).then_inc(score_exp_in, 1)
            dve.wait_ge(score_exp, 1)
            then(dve.tensor_reduce(exp_sum, exps, AX.X, ALU.add))
            then(dve.reciprocal(exp_inv, exp_sum))
            dve.tensor_tensor(score, exps, over_e(exp_inv), ALU.mult).then_inc(tok0_in, 1)
            dve.wait_ge(tok0_in, 1)

            def first_max(sc, most, hot):
                then(dve.tensor_reduce(most, sc, AX.X, ALU.max))
                tt(hot, sc, over_e(most), ALU.is_equal)
                ts(spare, hot[:, :, 0], -1.0, 1.0, ALU.mult, ALU.add)
                tt(hot[:, :, 1], hot[:, :, 1], spare, ALU.mult)
                tt(spare, spare, hot[:, :, 1], ALU.subtract)
                tt(hot[:, :, 2], hot[:, :, 2], spare, ALU.mult)

            def second(sc, hot, gone):
                ts(gone, hot, -4.0, None, ALU.mult)
                tt(gone, gone, sc, ALU.add)

            first_max(score, weight1, choice1)
            second(score, choice1, choice2)
            then(dve.tensor_reduce(weight2, choice2, AX.X, ALU.max))
            tt(spare, weight1, weight2, ALU.add)
            ts(spare, spare, 1e-8, None, ALU.add)
            then(dve.reciprocal(pair_inv, spare))
            ts(pair_inv, pair_inv, gates[:, 1:2], None, ALU.mult)
            tt(weight1, weight1, pair_inv, ALU.mult)
            tt(weight2, weight2, pair_inv, ALU.mult)
            dve.wait_ge(tok0_mm, 1)
            then(dve.tensor_copy(score0.rearrange("p b e -> p (b e)"), sbank[:, 128:128 + B * NX]))
            first_max(score0, top, choice1)
            second(score0, choice1, score0_rest)
            first_max(score0_rest, top, choice2)
            tt(choice1, choice1, over_e(weight1), ALU.mult)
            tt(choice2, choice2, over_e(weight2), ALU.mult)
            dve.tensor_tensor(coef[:, :, :], choice1, choice2, ALU.add).then_inc(coef_ok, 1)
            dve.wait_ge(coef_ok, 1)
            dve.wait_ge(b2_in, 16 * NX)

            def add_expert(s):
                for k in range(4):
                    u, e, b = s * 4 + k, s // 2, (s % 2) * 4 + k
                    if e >= 1:
                        dve.wait_ge(f_acc, (e - 1) * B + b + 1)
                    dve.scalar_tensor_tensor(out=xacc[:, b, :], in0=b2row[e], scalar=coef[:, b, e:e + 1],
                                             in1=xacc[:, b, :], op0=ALU.mult, op1=ALU.add).then_inc(f_bias, 1)
                    dve.wait_ge(f_bias, u + 1)
                    dve.wait_ge(f2, u + 1)
                    dve.scalar_tensor_tensor(out=xacc[:, b, :], in0=ybank[u % 2][:, :], scalar=coef[:, b, e:e + 1],
                                             in1=xacc[:, b, :], op0=ALU.mult, op1=ALU.add).then_inc(f_acc, 1)

            for s in range(2 * NX):
                add_expert(s)


_INS = ["x", "ctx_4096", "pos_BxS2", "mask_BxSxS2_ik0", "g_xattn", "g_ffn", "L0_xattn_Wq", "L0_xattn_Wk",
        "L0_xattn_Wv", "L0_xattn_Wo", "L0_ffn_gate_w", "L0_ffn_gate_b", "L0_ffn_w1", "L0_ffn_b1",
        "L0_ffn_w2", "L0_ffn_b2"]


def kernel(**inputs):
    import numpy as np
    import concourse.bacc as bacc
    from concourse.bass_utils import run_bass_kernel_spmd as run

    nc = bacc.Bacc("TRN2", target_bir_lowering=False, num_devices=1)
    arrays, args = {}, []
    for name in _INS:
        a = np.ascontiguousarray(inputs[name])
        arrays[f"in_{name}"] = a
        args.append(nc.dram_tensor(f"in_{name}", a.shape, mybir.dt.from_np(a.dtype), kind="ExternalInput").ap())
    freq = np.float32(1) / np.power(np.float32(10000.0), np.arange(0, D, 2, dtype=np.float32) / np.float32(D))
    angle = np.arange(MAX_POS, dtype=np.float32)[:, None] * freq[None, :]
    table = np.concatenate([np.cos(angle), np.cos(angle), np.sin(angle), -np.sin(angle)], axis=1)
    arrays["rope_rows"] = table
    rope_rows = nc.dram_tensor("rope_rows", table.shape, F32, kind="ExternalInput").ap()
    kv_scratch = nc.dram_tensor("kv_scratch", (KVH, B, P, 4, P), F32, kind="Internal").ap()
    out = nc.dram_tensor("out", (B, P, E), F32, kind="ExternalOutput").ap()
    build(nc, *args, rope_rows, kv_scratch, out)
    r = run(nc, [arrays], core_ids=[0])
    return r.results[0]["out"]
```
